# Optimizing a Trainium2 kernel written in Bass

```python
import numpy as np
import jax
import jax.numpy as jnp

def _softmax(x, axis=-1):
    return jax.nn.softmax(x, axis=axis)

def _gelu(x):
    return jax.nn.gelu(x, approximate=True)

def _silu(x):
    return jax.nn.silu(x)

def _sigmoid(x):
    return jax.nn.sigmoid(x)

def _layernorm(x, axis=-1, eps=1e-05):
    m = jnp.mean(x, axis=axis, keepdims=True)
    v = jnp.var(x, axis=axis, keepdims=True)
    return (x - m) / jnp.sqrt(v + eps)

def _scatter_add(tgt, idx, src, axis=0):
    return tgt.at[idx].add(src)

def _segment_sum(src, seg, n):
    return jax.ops.segment_sum(src, seg, n)
kernel_name = 'mk_adj_resnorm_d4_adj_r2_883c02'

def setup_inputs(seed: int=0):
    np.random.seed(seed)
    _w = jnp.asarray

    def _rec_inputs():
        import jax
        import jax.numpy as jnp
        _gk = jax.random.key(seed)
        x = -0.0002928 + 1 * jax.random.normal(jax.random.fold_in(_gk, 1), (32, 256, 128), jnp.float32)
        _a = jax.random.bernoulli(jax.random.fold_in(_gk, 2), 0.0625, (32, 256, 256))
        _a = jnp.logical_or(_a, jnp.swapaxes(_a, -1, -2))
        _a = jnp.logical_or(_a, jnp.eye(256, dtype=bool))
        _af = _a.astype(jnp.float32)
        _af = _af * jax.random.uniform(jax.random.fold_in(_gk, 3), (32, 256, 256), jnp.float32, 0.05, 1)
        adj = _af
        _nm = jnp.ones((32, 256), dtype=bool)
        nodemask = jnp.where(_nm, 1.0, 0.0).astype(jnp.int32)
        return (x, adj, nodemask)
    x, adj, nodemask = _rec_inputs()

    def _L0_gnn_setup():
        import jax, jax.numpy as jnp
        import numpy as np
        D_IN = 128
        D_OUT = 128
        key = jax.random.key(seed)
        k1, k2, k3 = jax.random.split(key, 3)
        B, N = (4, 2048)
        seq = jax.random.normal(k1, (B, N, D_IN), dtype=jnp.float32)
        adj = jax.random.uniform(k2, (B, N, N), dtype=jnp.float32)
        limit = float(np.sqrt(6.0 / (D_IN + D_OUT)))
        W = jax.random.uniform(k3, (D_IN, D_OUT), dtype=jnp.float32, minval=-limit, maxval=limit)
        bias = jnp.zeros((D_OUT,), dtype=jnp.float32)
        prelu_a = jnp.array(0.25, dtype=jnp.float32)
        return {'seq': seq, 'adj': adj, 'W': W, 'bias': bias, 'prelu_a': prelu_a}
    _L0_gnn_all = _L0_gnn_setup()
    _L0_gnn_in = {k: v for k, v in _L0_gnn_all.items() if k in ('W', 'bias', 'prelu_a')}
    del _L0_gnn_all

    def _L1_gnn_setup():
        import jax, jax.numpy as jnp
        import numpy as np
        D_IN = 128
        D_HID = 256
        key = jax.random.key(seed)
        k1, k2, k3, k4, k5, k6 = jax.random.split(key, 6)
        x = jax.random.normal(k1, (8, 2048, D_IN), dtype=jnp.float32)
        adj = jax.random.uniform(k2, (8, 2048, 2048), dtype=jnp.float32)
        s1 = 1.0 / np.sqrt(D_IN)
        s2 = 1.0 / np.sqrt(D_HID)
        W1 = jax.random.uniform(k3, (D_IN, D_HID), dtype=jnp.float32, minval=-s1, maxval=s1)
        b1 = jax.random.uniform(k4, (D_HID,), dtype=jnp.float32, minval=-s1, maxval=s1)
        W2 = jax.random.uniform(k5, (D_HID, D_IN), dtype=jnp.float32, minval=-s2, maxval=s2)
        b2 = jax.random.uniform(k6, (D_IN,), dtype=jnp.float32, minval=-s2, maxval=s2)
        eps = jnp.zeros((1,), dtype=jnp.float32)
        return {'x': x, 'adj': adj, 'eps': eps, 'W1': W1, 'b1': b1, 'W2': W2, 'b2': b2}
    _L1_gnn_all = _L1_gnn_setup()
    _L1_gnn_in = {k: v for k, v in _L1_gnn_all.items() if k in ('eps', 'W1', 'b1', 'W2', 'b2')}
    del _L1_gnn_all

    def _L2_gnn_setup():
        import jax, jax.numpy as jnp
        import numpy as np
        HIDDEN = 128
        NEG_INF = -1e+30
        key = jax.random.key(seed)
        k1, k2, k3, k4 = jax.random.split(key, 4)
        B, S, H = (4, 2048, HIDDEN)
        matrix = jax.random.normal(k1, (B, S, H), dtype=jnp.float32)
        mask = jax.random.randint(k2, (B, S), 0, 2, dtype=jnp.int32)
        adj = jax.random.uniform(k3, (B, S, S), dtype=jnp.float32)
        limit = float(np.sqrt(6.0 / (H + H)))
        W = jax.random.uniform(k4, (H, H), dtype=jnp.float32, minval=-limit, maxval=limit)
        return {'matrix': matrix, 'mask': mask, 'adj': adj, 'W': W}
    _L2_gnn_all = _L2_gnn_setup()
    _L2_gnn_in = {k: v for k, v in _L2_gnn_all.items() if k in ('W',)}
    del _L2_gnn_all

    def _L3_gnn_setup():
        import jax, jax.numpy as jnp
        import numpy as np
        from jax import lax
        DIM = 128
        EPS = 1e-05

        def _bn(h, g, b, m, v):
            scale = g / jnp.sqrt(v + EPS)
            return h * scale[None, :, None] + (b - m * scale)[None, :, None]

        def _conv1d(h, w, pad):
            return lax.conv_general_dilated(h, w, window_strides=(1,), padding=[(pad, pad)], dimension_numbers=('NCH', 'OIH', 'NCH'))
        key = jax.random.key(seed)
        ks = jax.random.split(key, 16)
        bs, n, d = (16, 1024, DIM)
        s = 0.05
        return {'x': jax.random.normal(ks[0], (bs, n, d), jnp.float32), 'mask': jnp.ones((bs, n, n), jnp.float32), 'w_se': jax.random.normal(ks[1], (3, d), jnp.float32) * s, 'b_se': jnp.zeros((3,), jnp.float32), 'conv1_w': jax.random.normal(ks[2], (d, d, 1), jnp.float32) * s, 'bn1_g': jnp.ones((d,), jnp.float32), 'bn1_b': jnp.zeros((d,), jnp.float32), 'bn1_m': jnp.zeros((d,), jnp.float32), 'bn1_v': jnp.ones((d,), jnp.float32), 'conv2_w': jax.random.normal(ks[3], (d, d, 17), jnp.float32) * s, 'bn2_g': jnp.ones((d,), jnp.float32), 'bn2_b': jnp.zeros((d,), jnp.float32), 'bn2_m': jnp.zeros((d,), jnp.float32), 'bn2_v': jnp.ones((d,), jnp.float32), 'w_msg': jax.random.normal(ks[4], (d, d), jnp.float32) * s, 'b_msg': jnp.zeros((d,), jnp.float32), 'w_ih': jax.random.normal(ks[5], (3 * d, 2 * d), jnp.float32) * s, 'b_ih': jnp.zeros((3 * d,), jnp.float32), 'w_hh': jax.random.normal(ks[6], (3 * d, d), jnp.float32) * s, 'b_hh': jnp.zeros((3 * d,), jnp.float32)}
    _L3_gnn_all = _L3_gnn_setup()
    _L3_gnn_in = {k: v for k, v in _L3_gnn_all.items() if k in ('w_se', 'b_se', 'conv1_w', 'bn1_g', 'bn1_b', 'bn1_m', 'bn1_v', 'conv2_w', 'bn2_g', 'bn2_b', 'bn2_m', 'bn2_v', 'w_msg', 'b_msg', 'w_ih', 'b_ih', 'w_hh', 'b_hh')}
    del _L3_gnn_all
    return {'x': x, 'adj': adj, 'nodemask': nodemask, 'L0_gnn_W': _L0_gnn_in['W'], 'L0_gnn_bias': _L0_gnn_in['bias'], 'L0_gnn_prelu_a': _L0_gnn_in['prelu_a'], 'L1_gnn_eps': _L1_gnn_in['eps'], 'L1_gnn_W1': _L1_gnn_in['W1'], 'L1_gnn_b1': _L1_gnn_in['b1'], 'L1_gnn_W2': _L1_gnn_in['W2'], 'L1_gnn_b2': _L1_gnn_in['b2'], 'L2_gnn_W': _L2_gnn_in['W'], 'L3_gnn_w_se': _L3_gnn_in['w_se'], 'L3_gnn_b_se': _L3_gnn_in['b_se'], 'L3_gnn_conv1_w': _L3_gnn_in['conv1_w'], 'L3_gnn_bn1_g': _L3_gnn_in['bn1_g'], 'L3_gnn_bn1_b': _L3_gnn_in['bn1_b'], 'L3_gnn_bn1_m': _L3_gnn_in['bn1_m'], 'L3_gnn_bn1_v': _L3_gnn_in['bn1_v'], 'L3_gnn_conv2_w': _L3_gnn_in['conv2_w'], 'L3_gnn_bn2_g': _L3_gnn_in['bn2_g'], 'L3_gnn_bn2_b': _L3_gnn_in['bn2_b'], 'L3_gnn_bn2_m': _L3_gnn_in['bn2_m'], 'L3_gnn_bn2_v': _L3_gnn_in['bn2_v'], 'L3_gnn_w_msg': _L3_gnn_in['w_msg'], 'L3_gnn_b_msg': _L3_gnn_in['b_msg'], 'L3_gnn_w_ih': _L3_gnn_in['w_ih'], 'L3_gnn_b_ih': _L3_gnn_in['b_ih'], 'L3_gnn_w_hh': _L3_gnn_in['w_hh'], 'L3_gnn_b_hh': _L3_gnn_in['b_hh']}

def reference(x, adj, nodemask, L0_gnn_W, L0_gnn_bias, L0_gnn_prelu_a, L1_gnn_eps, L1_gnn_W1, L1_gnn_b1, L1_gnn_W2, L1_gnn_b2, L2_gnn_W, L3_gnn_w_se, L3_gnn_b_se, L3_gnn_conv1_w, L3_gnn_bn1_g, L3_gnn_bn1_b, L3_gnn_bn1_m, L3_gnn_bn1_v, L3_gnn_conv2_w, L3_gnn_bn2_g, L3_gnn_bn2_b, L3_gnn_bn2_m, L3_gnn_bn2_v, L3_gnn_w_msg, L3_gnn_b_msg, L3_gnn_w_ih, L3_gnn_b_ih, L3_gnn_w_hh, L3_gnn_b_hh):
    import jax
    import jax.numpy as jnp

    def _L0_gnn_ref(seq, adj, W, bias, prelu_a):
        import jax, jax.numpy as jnp
        import numpy as np
        D_IN = 128
        D_OUT = 128
        seq_fts = jnp.einsum('bnd,de->bne', seq, W)
        out = jnp.einsum('bnm,bme->bne', adj, seq_fts) + bias
        return jnp.where(out >= 0, out, prelu_a * out)

    def _L1_gnn_ref(x, adj, eps, W1, b1, W2, b2):
        import jax, jax.numpy as jnp
        import numpy as np
        D_IN = 128
        D_HID = 256
        aggregated = jnp.einsum('bnm,bmd->bnd', adj, x)
        h = (1.0 + eps) * x + aggregated
        h = jax.nn.relu(h @ W1 + b1)
        return h @ W2 + b2

    def _L2_gnn_ref(matrix, mask, adj, W):
        import jax, jax.numpy as jnp
        import numpy as np
        HIDDEN = 128
        NEG_INF = -1e+30
        intermediate = jnp.einsum('bsh,hd->bsd', matrix, W)
        similarities = jnp.einsum('bsd,btd->bst', intermediate, matrix)
        similarities = similarities * adj
        key_mask = mask[:, None, :].astype(bool)
        masked = jnp.where(key_mask, similarities, NEG_INF)
        attn = jax.nn.softmax(masked, axis=-1)
        output = jnp.einsum('bst,bth->bsh', attn, matrix)
        return output

    def _L3_gnn_ref(x, mask, w_se, b_se, conv1_w, bn1_g, bn1_b, bn1_m, bn1_v, conv2_w, bn2_g, bn2_b, bn2_m, bn2_v, w_msg, b_msg, w_ih, b_ih, w_hh, b_hh):
        import jax, jax.numpy as jnp
        import numpy as np
        from jax import lax
        DIM = 128
        EPS = 1e-05

        def _bn(h, g, b, m, v):
            scale = g / jnp.sqrt(v + EPS)
            return h * scale[None, :, None] + (b - m * scale)[None, :, None]

        def _conv1d(h, w, pad):
            return lax.conv_general_dilated(h, w, window_strides=(1,), padding=[(pad, pad)], dimension_numbers=('NCH', 'OIH', 'NCH'))
        d = x.shape[-1]
        xc = jnp.transpose(x, (0, 2, 1))
        h = _bn(_conv1d(xc, conv1_w, 0), bn1_g, bn1_b, bn1_m, bn1_v)
        h = jax.nn.relu(h)
        h = _bn(_conv1d(h, conv2_w, 8), bn2_g, bn2_b, bn2_m, bn2_v)
        x_conv = jnp.transpose(jax.nn.relu(h + xc), (0, 2, 1))
        s = x @ w_se.T + b_se
        sq = jnp.sum(s * s, axis=-1)
        dist = sq[:, :, None] + sq[:, None, :] - 2.0 * jnp.einsum('bnd,bmd->bnm', s, s)
        A = jnp.exp(-dist) * mask
        msg = jax.nn.relu(x @ w_msg.T + b_msg)
        x_nmp = jnp.einsum('bnm,bmd->bnd', A, msg)
        x_in = jnp.concatenate([x_conv, x_nmp], axis=-1)
        gi = x_in @ w_ih.T + b_ih
        gh = x @ w_hh.T + b_hh
        gi_r, gi_z, gi_n = (gi[..., :d], gi[..., d:2 * d], gi[..., 2 * d:])
        gh_r, gh_z, gh_n = (gh[..., :d], gh[..., d:2 * d], gh[..., 2 * d:])
        r = jax.nn.sigmoid(gi_r + gh_r)
        z = jax.nn.sigmoid(gi_z + gh_z)
        nn_ = jnp.tanh(gi_n + r * gh_n)
        return (1.0 - z) * nn_ + z * x
    x = _layernorm(x + _L0_gnn_ref(x, adj, L0_gnn_W, L0_gnn_bias, L0_gnn_prelu_a), axis=-1)
    x = _layernorm(x + _L1_gnn_ref(x, adj, L1_gnn_eps, L1_gnn_W1, L1_gnn_b1, L1_gnn_W2, L1_gnn_b2), axis=-1)
    x = _layernorm(x + _L2_gnn_ref(x, nodemask, adj, L2_gnn_W), axis=-1)
    x = _layernorm(x + _L3_gnn_ref(x, adj, L3_gnn_w_se, L3_gnn_b_se, L3_gnn_conv1_w, L3_gnn_bn1_g, L3_gnn_bn1_b, L3_gnn_bn1_m, L3_gnn_bn1_v, L3_gnn_conv2_w, L3_gnn_bn2_g, L3_gnn_bn2_b, L3_gnn_bn2_m, L3_gnn_bn2_v, L3_gnn_w_msg, L3_gnn_b_msg, L3_gnn_w_ih, L3_gnn_b_ih, L3_gnn_w_hh, L3_gnn_b_hh), axis=-1)
    return x

_drawn_inputs = setup_inputs


def setup_inputs(seed=0):
    import zlib

    import numpy as np

    out = dict(_drawn_inputs(seed))
    spreads = {'L0_gnn_bias': (0.0, 0.1),
     'L3_gnn_b_se': (0.0, 0.8),
     'L3_gnn_bn1_g': (1.0, 0.6),
     'L3_gnn_bn1_b': (0.0, 0.709),
     'L3_gnn_bn1_m': (0.0, 0.581),
     'L3_gnn_bn1_v': (1.0, 0.6),
     'L3_gnn_bn2_g': (1.0, 0.6),
     'L3_gnn_bn2_b': (0.0, 0.8),
     'L3_gnn_bn2_m': (0.0, 0.8),
     'L3_gnn_bn2_v': (1.0, 0.6),
     'L3_gnn_b_msg': (0.0, 0.1),
     'L3_gnn_b_ih': (0.0, 0.452),
     'L3_gnn_b_hh': (0.0, 0.557)}
    factors = {'L1_gnn_b1': 3.306}
    for name, (base, spread) in spreads.items():
        noise = np.random.default_rng([zlib.crc32(name.encode()), seed]).standard_normal(out[name].shape)
        drawn = base * np.exp(spread * noise) if base else spread * noise
        out[name] = jnp.asarray(drawn.astype(out[name].dtype))
    for name, factor in factors.items():
        out[name] = (out[name] * factor).astype(out[name].dtype)
    return out
```

```python
from contextlib import ExitStack

import concourse.bass as bass
from concourse import mybir
from concourse.alu_op_type import AluOpType as ALU

ACT = mybir.ActivationFunctionType
F32 = mybir.dt.float32
F32R = mybir.dt.float32r
BF16 = mybir.dt.bfloat16
I32 = mybir.dt.int32

P = 128
EPS = 1e-5
MASKED = -1e30
LOWEST = -3.0e38

VEC = ["prelu_a", "eps", "b1_lo", "b1_hi", "b_se", "bn1_g", "bn1_b", "bn1_m", "bn1_v",
       "bn2_g", "bn2_b", "bn2_m", "bn2_v", "ih_r", "ih_z", "ih_n", "hh_r", "hh_z", "hh_n"]
V = {name: i for i, name in enumerate(VEC)}
BIAS_ROWS = ["b0", "b2", "b_msg"]
S_ROWS, SQ_ROWS, ONE_ROWS, FEATS = 0, 32, 64, 96


def adjacency_block_kernel(nc, x, adj, adj_t, mask, vecs, bias_rows, w0, w1, w2, w_att, w_se, w_conv1,
                           w_conv2, w_msg, w_ih, w_hh, out):
    graphs, nodes, ch = x.shape
    pairs = graphs // 2
    blocks = 2 * nodes // P
    tiles = nodes // P
    cols = 2 * nodes
    taps = w_conv2.shape[1]
    pad = taps // 2
    assert ch == P and blocks == 4 and cols == 512

    x_d = x.rearrange("(k g) (t p) c -> k p (g t) c", g=2, p=P)
    adj_d = adj.rearrange("(k g) (t p) m -> k p (g t) m", g=2, p=P)
    adj_t_d = adj_t.rearrange("(k g) (t p) n -> k p (g t) n", g=2, p=P)
    mask_d = mask.rearrange("(k o g) n -> k o (g n)", g=2, o=1)
    out_d = out.rearrange("(k g) (t p) c -> k p (g t) c", g=2, p=P)

    with ExitStack() as ctx:
        def sb(name, shape, dt=F32):
            return ctx.enter_context(nc.sbuf_tensor(name, shape, dt))

        sems = {}

        def sem(name):
            if name not in sems:
                sems[name] = ctx.enter_context(nc.semaphore(name))
            return sems[name]

        def need(eng, name, count):
            if isinstance(count, int) and count <= 0:
                return
            eng.wait_ge(sem(name), count)

        def need_apart(eng, name, count):
            eng.wait_ge(sem("params"), 16)
            need(eng, name, count)

        class Pair:
            def __init__(self, eng, n):
                held = (lambda v: eng.snap(eng.to_reg(v))) if not isinstance(n, int) else (lambda v: v)
                self.n, self.prev, self.dma = held(n), held(n - 1), held(n * 16)
                self.prev_dma = held(n * 16 - 16)

        def over_pairs(eng, steps):
            steps(Pair(eng, 1), None)
            steps(Pair(eng, 2), Pair(eng, 1))
            with eng.Fori(3, pairs + 1) as f:
                steps(Pair(eng, f), Pair(eng, f - 1))
            steps(None, Pair(eng, pairs))

        vec = sb("vec", [P, len(VEC)])
        w0_sb = sb("w0_sb", [P, P])
        w1_sb = sb("w1_sb", [P, 2 * P])
        w2_sb = sb("w2_sb", [P, 2, P])
        watt_sb = sb("watt_sb", [P, P])
        wmsg_sb = sb("wmsg_sb", [P, P])
        n_split = P * (1 + 1 + taps + 9)
        w_raw = sb("w_raw", [P, n_split])
        w_hi = sb("w_hi", [P, n_split], F32R)
        w_lo = sb("w_lo", [P, n_split], F32R)
        bias_raw = sb("bias_raw", [FEATS, 3, P])
        bias_rest = sb("bias_rest", [FEATS, 3, P])
        bias_hi = sb("bias_hi", [FEATS, 3, P], BF16)
        bias_mid = sb("bias_mid", [FEATS, 3, P], BF16)
        bias_parts = sb("bias_parts", [FEATS, 3, P], BF16)
        ident = sb("ident", [P, P])
        self_diag = sb("self_diag", [P, P])
        ones_rows = sb("ones_rows", [FEATS, P], BF16)
        first_row = sb("first_row", [P, P], BF16)
        bn1_scale = sb("bn1_scale", [P, 1])
        bn1_shift = sb("bn1_shift", [P, 1])
        bn2_scale = sb("bn2_scale", [P, 1])
        bn2_shift = sb("bn2_shift", [P, 1])
        bn_tmp = sb("bn_tmp", [P, 4])
        minus_half = sb("minus_half", [P, 4])
        one_minus_a = sb("one_minus_a", [P, 1])
        half_br = sb("half_br", [P, 1])
        half_bz = sb("half_bz", [P, 1])

        x_in = sb("x_in", [P, blocks, P])
        adj_in = sb("adj_in", [P, blocks, nodes])
        adjt_in = sb("adjt_in", [P, blocks, nodes])
        mask_in = sb("mask_in", [P, cols], I32)
        unmasked = sb("unmasked", [P, 2, nodes])
        masked = sb("masked", [P, 2, nodes])
        mask_neg = sb("mask_neg", [P, 2, nodes], BF16)
        adj_m = sb("adj_m", [P, blocks, nodes])
        u0 = sb("u0", [P, cols])
        u1 = sb("u1", [P, cols])
        neg0 = sb("neg0", [P, cols])
        z = [sb(f"z{n}", [P, blocks, P]) for n in range(3)]
        res0 = sb("res0", [P, cols])
        x1 = sb("x1", [P, blocks, P])
        x2 = sb("x2", [P, blocks, P])
        x3 = sb("x3", [P, blocks, P])
        h1 = sb("h1", [P, 2, cols])
        x2t = sb("x2t", [P, cols])
        q = sb("q", [P, cols])
        prob = sb("prob", [P, blocks, nodes])
        expo = sb("expo", [P, blocks, nodes])
        expo_t = sb("expo_t", [P, blocks, nodes])
        row_max = sb("row_max", [P, blocks])
        minus_max = sb("minus_max", [P, blocks])
        row_sum = sb("row_sum", [P, blocks])
        row_inv = sb("row_inv", [P, blocks])
        bn6 = sb("bn6", [P, 4, blocks, 6])
        stats = sb("stats", [P, 4, blocks, 2])
        var_eps = sb("var_eps", [P, 4, blocks])
        rstd = sb("rstd", [P, 4, blocks])
        adjt_kept = sb("adjt_kept", [P, blocks, nodes])
        x3t = sb("x3t", [P, cols])
        x3h = sb("x3h", [P, cols], F32R)
        x3l = sb("x3l", [P, cols], F32R)
        hc = sb("hc", [P, 2, nodes])
        hch = sb("hch", [P, 2, nodes + 2 * pad], F32R)
        hcl = sb("hcl", [P, 2, nodes + 2 * pad], F32R)
        feat_r = sb("feat_r", [FEATS, cols])
        feat_l = sb("feat_l", [FEATS, cols])
        msg = sb("msg", [P, blocks, P])
        near = sb("near", [P, blocks, nodes])
        adj_near = sb("adj_near", [P, blocks, nodes])
        nmh = sb("nmh", [P, cols], F32R)
        nml = sb("nml", [P, cols], F32R)
        xc_pre = sb("xc_pre", [P, cols])
        xc = sb("xc", [P, cols])
        xch = sb("xch", [P, cols], F32R)
        xcl = sb("xcl", [P, cols], F32R)
        tr = sb("tr", [P, cols])
        tz = sb("tz", [P, cols])
        reset = sb("reset", [P, cols])
        gated = sb("gated", [P, cols])
        new_pre = sb("new_pre", [P, cols])
        new = sb("new", [P, cols])
        x_less_new = sb("x_less_new", [P, cols])
        x_plus_new = sb("x_plus_new", [P, cols])
        mixed = sb("mixed", [P, cols])
        y3t = sb("y3t", [P, cols])
        out_sb = sb("out_sb", [P, blocks, P])

        F = [ctx.enter_context(nc.psum_tensor(f"front{n}", [P, 512], F32)) for n in range(4)]
        B = [ctx.enter_context(nc.psum_tensor(f"back{n}", [P, 512], F32)) for n in range(4)]

        def block_of(t, k):
            return t[:, k * P:(k + 1) * P]

        def vcol(name):
            return vec[:, V[name]:V[name] + 1]

        SE, C1, C2, IH, HH = 0, 1, 2, 2 + taps, 2 + taps + 6

        block = ctx.enter_context(nc.Block())

        @block.sync
        def _(sp):
            sp.dma_start(vec[:, :], vecs).then_inc(sem("params"), 16)
            for dst, src in ((w0_sb[:, :], w0), (w1_sb[:, :], w1), (watt_sb[:, :], w_att),
                             (wmsg_sb[:, :], w_msg),
                             (w2_sb[:, :, :], w2.rearrange("(j p) c -> p j c", p=P))):
                sp.dma_start(dst, src).then_inc(sem("params"), 16)
            for row in (0, 32, 64):
                sp.dma_start(bias_raw[row:row + 1, :, :],
                             bias_rows.rearrange("(o r) c -> o r c", o=1)).then_inc(sem("bias_in"), 16)
            for at, src, count in ((SE, w_se, 1), (C1, w_conv1, 1), (C2, w_conv2, taps),
                                   (IH, w_ih, 6), (HH, w_hh, 3)):
                dst = w_raw[:, at * P:(at + count) * P]
                if count > 1:
                    dst = dst.rearrange("p (k c) -> p k c", k=count)
                sp.dma_start(dst, src).then_inc(sem("weights_in"), 16)

            def loads(f):
                need(sp, "res0", f.prev)
                sp.dma_start(x_in[:, :, :], x_d[f.prev]).then_inc(sem("x_in"), 16)
                need(sp, "adj_m", f.prev)
                sp.dma_start(mask_in[:, :], mask_d[f.prev].broadcast_to([P, cols])).then_inc(sem("mask_in"), 16)
                sp.dma_start(adj_in[:, :, :], adj_d[f.prev]).then_inc(sem("adj_in"), 16)
                need(sp, "u1_ps", f.prev)
                need(sp, "adjt_kept", f.prev)
                sp.dma_start(adjt_in[:, :, :], adj_t_d[f.prev]).then_inc(sem("adjt_in"), 16)

            def store(b):
                need(sp, "out_rows", b.n)
                sp.dma_start(out_d[b.prev], out_sb[:, :, :]).then_inc(sem("stored"), 16)

            loads(Pair(sp, 1))
            loads(Pair(sp, 2))
            with sp.Fori(3, pairs + 1) as k:
                loads(Pair(sp, k))
                store(Pair(sp, k - 2))
            store(Pair(sp, pairs - 1))
            store(Pair(sp, pairs))
            sp.wait_ge(sem("stored"), 16 * pairs)

        @block.gpsimd
        def _(pool):
            pool.memset(ident[:, :], 0.0).then_inc(sem("pool_init"), 1)
            pool.memset(minus_half[:, :], -0.5)
            pool.memset(ones_rows[:, :], 1.0)
            pool.memset(first_row[:, :], 0.0)
            pool.memset(feat_l[:, :], 1.0)
            pool.memset(feat_r[:, :], 1.0)
            pool.memset(hch[:, :, :].bitcast(F32), 0.0)
            pool.memset(hcl[:, :, :].bitcast(F32), 0.0).then_inc(sem("pool_init"), 1)
            pool.wait_ge(sem("pool_init"), 2)
            pool.memset(first_row[0:1, :], 1.0).then_inc(sem("pool_init"), 1)
            pool.affine_select(out=ident[:, :], in_=ident[:, :], compare_op=ALU.not_equal, fill=1.0,
                               base=0, pattern=[[-1, P]], channel_multiplier=1).then_inc(sem("pool_init"), 1)
            pool.wait_ge(sem("bn_var"), 1)
            pool.tensor_tensor(bn_tmp[:, 2:4], bn_tmp[:, 0:2], minus_half[:, 0:2], ALU.pow)\
                .then_inc(sem("bn_rstd"), 1)

            def front_masks(f):
                need_apart(pool, "mask_in", f.dma)
                need(pool, "soft_in", f.prev)
                pool.tensor_scalar(masked[:, :, :], mask_in[:, :].rearrange("p (g n) -> p g n", g=2),
                                   0.0, None, ALU.is_equal).then_inc(sem("masked"), 1)
                need_apart(pool, "masked", f.n)
                pool.tensor_scalar(unmasked[:, :, :], masked[:, :, :], -1.0, 1.0, ALU.mult, ALU.add)
                pool.tensor_scalar(mask_neg[:, :, :], masked[:, :, :], MASKED, None, ALU.mult)\
                    .then_inc(sem("mask_neg"), 1)
                need(pool, "mask_neg", f.n)
                need(pool, "adj_in", f.dma)
                for g in range(2):
                    at = slice(tiles * g, tiles * (g + 1))
                    keep = unmasked[:, g:g + 1, :].broadcast_to([P, tiles, nodes])
                    op = pool.tensor_tensor(adj_m[:, at, :], adj_in[:, at, :], keep, ALU.mult)
                op.then_inc(sem("adj_keep"), 1)
                need(pool, "adj_keep", f.n)
                for g in range(2):
                    at = slice(tiles * g, tiles * (g + 1))
                    fill = masked[:, g:g + 1, :].broadcast_to([P, tiles, nodes])
                    op = pool.tensor_tensor(adj_m[:, at, :], adj_m[:, at, :], fill, ALU.add)
                op.then_inc(sem("adj_m"), 1)

            def rsqrt(n, k):
                need(pool, f"var{n}", k.n)
                pool.tensor_tensor(rstd[:, n, :], var_eps[:, n, :], minus_half[:, 0:blocks], ALU.pow)\
                    .then_inc(sem(f"rstd{n}"), 1)

            def low_part(low, whole, high, name, k, ready):
                need(pool, ready, k.n)
                pool.tensor_tensor(low, whole, high.bitcast(F32), ALU.subtract).then_inc(sem(name), 1)

            def keep_adjt(f):
                need_apart(pool, "adj_near", f.prev)
                need(pool, "adjt_in", f.dma)
                pool.tensor_scalar(adjt_kept[:, :, :], adjt_in[:, :, :], 1.0, None, ALU.mult)\
                    .then_inc(sem("adjt_kept"), 1)

            def steps(f, b):
                if f is not None:
                    front_masks(f)
                if b is not None:
                    low_part(x3l[:, :], x3t[:, :], x3h[:, :], "x3_parts", b, "x3_high")
                if f is not None:
                    rsqrt(0, f)
                if b is not None:
                    low_part(hcl[:, :, pad:pad + nodes], hc[:, :, :], hch[:, :, pad:pad + nodes],
                             "hc_parts", b, "hc_high")
                    need_apart(pool, "feat_s", b.n)
                    need(pool, "dist", b.prev)
                    pool.tensor_scalar(feat_l[0:32, :], feat_r[0:32, :], -2.0, None, ALU.mult)\
                        .then_inc(sem("feat_l"), 1)
                if f is not None:
                    keep_adjt(f)
                    rsqrt(1, f)
                if b is not None:
                    low_part(xcl[:, :], xc[:, :], xch[:, :], "xc_parts", b, "xc_high")
                if f is not None:
                    rsqrt(2, f)
                if b is not None:
                    need(pool, "new", b.n)
                    pool.tensor_tensor(x_less_new[:, :], x3t[:, :], new[:, :], ALU.subtract)\
                        .then_inc(sem("x_less_new"), 1)
                    pool.tensor_tensor(x_plus_new[:, :], x3t[:, :], new[:, :], ALU.add)\
                        .then_inc(sem("x_plus_new"), 1)
                    rsqrt(3, b)

            over_pairs(pool, steps)

        @block.scalar
        def _(act):
            act.wait_ge(sem("gate_bias"), 1)

            def steps(f, b):
                if b is not None:
                    need(act, "x3t_ps", b.n)
                    act.activation(x3t[:, :], B[1][:, :], ACT.Copy).then_inc(sem("x3t"), 1)
                if f is not None:
                    need(act, "u0_ps", f.n)
                    act.activation(u0[:, :], F[2][:, :], ACT.Copy).then_inc(sem("u0"), 1)
                if b is not None:
                    need(act, "conv1", b.n)
                    act.activation(hc[:, :, :], B[2][:, :].rearrange("p (g n) -> p g n", g=2), ACT.Relu,
                                   bias=bn1_shift[:, :], scale=bn1_scale[:, :]).then_inc(sem("hc"), 1)
                if f is not None:
                    need(act, "y0", f.n)
                    act.activation(neg0[:, :], F[3][:, :], ACT.Relu, scale=-1.0).then_inc(sem("neg0"), 1)
                if b is not None:
                    need(act, "s_ps", b.n)
                    act.activation(feat_r[0:64, :], B[3][0:64, :], ACT.Identity,
                                   bias=vec[0:64, V["b_se"]:V["b_se"] + 1]).then_inc(sem("feat_s"), 1)
                    act.activation(feat_l[64:96, :], B[3][64:96, :], ACT.Square,
                                   bias=vec[64:96, V["b_se"]:V["b_se"] + 1]).then_inc(sem("feat_sq"), 1)
                    need(act, "msg_ps", b.n)
                    act.activation(msg[:, :, :], B[1][:, :].rearrange("p (k c) -> p k c", k=blocks),
                                   ACT.Relu).then_inc(sem("msg"), 1)
                    need(act, "dist", b.n)
                    for g in range(2):
                        act.activation(near[:, tiles * g:tiles * (g + 1), :],
                                       B[2 + g][:, :].rearrange("p (t n) -> p t n", t=tiles),
                                       ACT.Exp, scale=-1.0).then_inc(sem(f"near{g}"), 1)
                if f is not None:
                    need(act, "u1_ps", f.n)
                    act.activation(u1[:, :], F[2][:, :], ACT.Copy).then_inc(sem("u1c"), 1)
                if b is not None:
                    need(act, "nmp", b.n)
                    act.activation(nmh[:, :], B[1][:, :], ACT.Copy).then_inc(sem("nm_high"), 1)
                if f is not None:
                    for j in range(2):
                        need(act, f"h1_ps{j}", f.n)
                        act.activation(h1[:, j, :], F[j][:, :], ACT.Relu,
                                       bias=vcol("b1_lo" if j == 0 else "b1_hi")).then_inc(sem(f"h1_{j}"), 1)
                    need(act, "x2t_ps", f.n)
                    act.activation(x2t[:, :], F[2][:, :], ACT.Copy).then_inc(sem("x2t"), 1)
                    need(act, "q_ps", f.n)
                    act.activation(q[:, :], F[3][:, :], ACT.Copy).then_inc(sem("q"), 1)
                if b is not None:
                    need(act, "xc_pre", b.n)
                    act.activation(xc[:, :], xc_pre[:, :], ACT.Relu, bias=bn2_shift[:, :])\
                        .then_inc(sem("xc"), 1)
                if f is not None:
                    need(act, "soft_in", f.n)
                    for k in range(blocks):
                        op = act.activation(expo[:, k, :], prob[:, k, :], ACT.Exp,
                                            bias=minus_max[:, k:k + 1], accum_out=row_sum[:, k:k + 1])
                    op.then_inc(sem("expo"), 1)
                    need(act, "expo_t_ps", f.n)
                    act.activation(expo_t[:, 0:2, :], F[2][:, :].rearrange("p (t n) -> p t n", t=tiles),
                                   ACT.Copy).then_inc(sem("expo_t0"), 1)
                if b is not None:
                    need(act, "gates_ps", b.n)
                    act.activation(tr[:, :], B[2][:, :], ACT.Tanh, bias=half_br[:, :], scale=0.5)\
                        .then_inc(sem("tr"), 1)
                    act.activation(tz[:, :], B[3][:, :], ACT.Tanh, bias=half_bz[:, :], scale=0.5)\
                        .then_inc(sem("tz"), 1)
                    need(act, "new_pre", b.n)
                    act.activation(new[:, :], new_pre[:, :], ACT.Tanh, bias=vcol("ih_n"))\
                        .then_inc(sem("new"), 1)

            over_pairs(act, steps)

        @block.vector
        def _(dve):
            dve.wait_ge(sem("params"), 16 * 6)
            for n, name in enumerate(("bn1_v", "bn2_v")):
                op = dve.tensor_scalar(bn_tmp[:, n:n + 1], vcol(name), EPS, None, ALU.add)
            op.then_inc(sem("bn_var"), 1)
            dve.tensor_scalar(one_minus_a[:, :], vcol("prelu_a"), -1.0, 1.0, ALU.mult, ALU.add)
            dve.tensor_tensor(half_br[:, :], vcol("ih_r"), vcol("hh_r"), ALU.add)
            dve.tensor_tensor(half_bz[:, :], vcol("ih_z"), vcol("hh_z"), ALU.add).then_inc(sem("dve_init"), 1)
            dve.wait_ge(sem("dve_init"), 1)
            dve.tensor_scalar(half_br[:, :], half_br[:, :], 0.5, None, ALU.mult)
            dve.tensor_scalar(half_bz[:, :], half_bz[:, :], 0.5, None, ALU.mult).then_inc(sem("dve_init"), 1)
            dve.wait_ge(sem("bn_rstd"), 1)
            dve.tensor_tensor(bn1_scale[:, :], vcol("bn1_g"), bn_tmp[:, 2:3], ALU.mult)
            dve.tensor_tensor(bn2_scale[:, :], vcol("bn2_g"), bn_tmp[:, 3:4], ALU.mult).then_inc(sem("dve_init"), 1)
            dve.wait_ge(sem("dve_init"), 3)
            dve.tensor_tensor(bn1_shift[:, :], vcol("bn1_m"), bn1_scale[:, :], ALU.mult)
            dve.tensor_tensor(bn2_shift[:, :], vcol("bn2_m"), bn2_scale[:, :], ALU.mult).then_inc(sem("dve_init"), 1)
            dve.wait_ge(sem("dve_init"), 4)
            dve.tensor_tensor(bn1_shift[:, :], vcol("bn1_b"), bn1_shift[:, :], ALU.subtract)
            dve.tensor_tensor(bn2_shift[:, :], vcol("bn2_b"), bn2_shift[:, :], ALU.subtract)\
                .then_inc(sem("gate_bias"), 1)
            dve.wait_ge(sem("pool_init"), 4)
            dve.tensor_scalar(self_diag[:, :], ident[:, :], vcol("eps"), None, ALU.mult).then_inc(sem("dve_init"), 1)
            dve.wait_ge(sem("dve_init"), 5)
            dve.tensor_tensor(self_diag[:, :], self_diag[:, :], ident[:, :], ALU.add).then_inc(sem("self_diag"), 1)
            dve.memset(bias_parts[:, :, :], 0.0).then_inc(sem("dve_init"), 1)
            dve.wait_ge(sem("bias_in"), 16 * 3)
            for row in (0, 32, 64):
                op = dve.tensor_copy(bias_hi[row:row + 1, :, :], bias_raw[row:row + 1, :, :])
            op.then_inc(sem("dve_init"), 1)
            dve.wait_ge(sem("dve_init"), 7)
            dve.tensor_copy(bias_parts[0:1, :, :], bias_hi[0:1, :, :])
            for row in (32, 64):
                op = dve.tensor_tensor(bias_rest[row:row + 1, :, :], bias_raw[row:row + 1, :, :],
                                       bias_hi[row:row + 1, :, :], ALU.subtract)
            op.then_inc(sem("dve_init"), 1)
            dve.wait_ge(sem("dve_init"), 8)
            dve.tensor_copy(bias_parts[32:33, :, :], bias_rest[32:33, :, :])
            dve.tensor_copy(bias_mid[64:65, :, :], bias_rest[64:65, :, :]).then_inc(sem("dve_init"), 1)
            dve.wait_ge(sem("dve_init"), 9)
            dve.tensor_tensor(bias_parts[64:65, :, :], bias_rest[64:65, :, :], bias_mid[64:65, :, :],
                              ALU.subtract).then_inc(sem("bias_parts"), 1)
            dve.wait_ge(sem("weights_in"), 16 * 5)
            dve.tensor_copy(w_hi[:, :], w_raw[:, :]).then_inc(sem("w_high"), 1)
            dve.wait_ge(sem("w_high"), 1)
            dve.tensor_tensor(w_lo[:, :], w_raw[:, :], w_hi[:, :].bitcast(F32), ALU.subtract)\
                .then_inc(sem("w_parts"), 1)

            def statistics(n, src, k):
                for i in range(blocks):
                    op = dve.bn_stats(bn6[:, n, i, :], src(i))
                op.then_inc(sem(f"bn6_{n}"), 1)
                need_apart(dve, f"bn6_{n}", k.n)
                for i in range(blocks):
                    op = dve.bn_aggr(stats[:, n, i, :], bn6[:, n, i, :])
                op.then_inc(sem(f"stats{n}"), 1)
                need(dve, f"stats{n}", k.n)
                dve.tensor_scalar(var_eps[:, n, :], stats[:, n, :, 1], EPS, None, ALU.add)\
                    .then_inc(sem(f"var{n}"), 1)

            def normalize(n, dst, src, k, name):
                need(dve, f"rstd{n}", k.n)
                for i in range(blocks):
                    op = dve.tensor_scalar(dst[:, i, :], src(i), stats[:, n, i, 0:1], rstd[:, n, i:i + 1],
                                           ALU.subtract, ALU.mult)
                op.then_inc(sem(name), 1)

            def steps(f, b):
                if b is not None:
                    need(dve, "x3t", b.n)
                    dve.tensor_copy(x3h[:, :], x3t[:, :]).then_inc(sem("x3_high"), 1)
                if f is not None:
                    need(dve, "neg0", f.n)
                    dve.scalar_tensor_tensor(out=res0[:, :], in0=neg0[:, :], scalar=one_minus_a[:, :],
                                             in1=x_in[:, :, :].rearrange("p k c -> p (k c)"),
                                             op0=ALU.mult, op1=ALU.add).then_inc(sem("res0"), 1)
                    need(dve, "res0", f.n)
                    dve.tensor_tensor(z[0][:, :, :].rearrange("p k c -> p (k c)"), F[3][:, :], res0[:, :],
                                      ALU.add).then_inc(sem("z0"), 1)
                    need(dve, "z0", f.n)
                    statistics(0, lambda i: z[0][:, i, :], f)
                if b is not None:
                    need(dve, "hc", b.n)
                    dve.tensor_copy(hch[:, :, pad:pad + nodes], hc[:, :, :]).then_inc(sem("hc_high"), 1)
                if f is not None:
                    normalize(0, x1, lambda i: z[0][:, i, :], f, "x1")
                if b is not None:
                    need(dve, "feat_s", b.n)
                    dve.tensor_tensor(feat_r[32:64, :], feat_r[32:64, :], feat_r[32:64, :], ALU.mult)\
                        .then_inc(sem("feat_r"), 1)
                    for g in range(2):
                        need(dve, f"near{g}", b.n)
                        need(dve, "adjt_kept", b.n)
                        at = slice(tiles * g, tiles * (g + 1))
                        op = dve.tensor_tensor(adj_near[:, at, :], near[:, at, :], adjt_kept[:, at, :],
                                               ALU.mult)
                    op.then_inc(sem("adj_near"), 1)
                    need(dve, "nm_high", b.n)
                    dve.tensor_tensor(nml[:, :], B[1][:, :], nmh[:, :].bitcast(F32), ALU.subtract)\
                        .then_inc(sem("nm_parts"), 1)
                if f is not None:
                    need(dve, "y1", f.n)
                    dve.tensor_tensor(z[1][:, :, :].rearrange("p k c -> p (k c)"), F[3][:, :],
                                      x1[:, :, :].rearrange("p k c -> p (k c)"), ALU.add)\
                        .then_inc(sem("z1"), 1)
                    need(dve, "z1", f.n)
                    statistics(1, lambda i: z[1][:, i, :], f)
                    normalize(1, x2, lambda i: z[1][:, i, :], f, "x2")
                if b is not None:
                    need(dve, "conv2", b.n)
                    dve.scalar_tensor_tensor(out=xc_pre[:, :], in0=B[0][:, :], scalar=bn2_scale[:, :],
                                             in1=x3t[:, :], op0=ALU.mult, op1=ALU.add)\
                        .then_inc(sem("xc_pre"), 1)
                    need(dve, "xc", b.n)
                    dve.tensor_copy(xch[:, :], xc[:, :]).then_inc(sem("xc_high"), 1)
                if f is not None:
                    need_apart(dve, "scores", f.n)
                    need(dve, "adj_m", f.n)
                    for k in range(blocks):
                        g, t = divmod(k, tiles)
                        op = dve.tensor_tensor_reduce(out=prob[:, k, :], in0=F[g][:, t * nodes:(t + 1) * nodes],
                                                      in1=adj_m[:, k, :], scale=1.0, scalar=LOWEST,
                                                      op0=ALU.mult, op1=ALU.max,
                                                      accum_out=row_max[:, k:k + 1])
                    op.then_inc(sem("prob"), 1)
                    need(dve, "prob", f.n)
                    dve.tensor_scalar(minus_max[:, :], row_max[:, :], -1.0, None, ALU.mult)\
                        .then_inc(sem("soft_in"), 1)
                    need(dve, "expo", f.n)
                    dve.reciprocal(row_inv[:, :], row_sum[:, :]).then_inc(sem("row_inv"), 1)
                    need(dve, "expo_t_ps", f.n)
                    dve.tensor_copy(expo_t[:, 2:4, :], F[3][:, :].rearrange("p (t n) -> p t n", t=tiles))\
                        .then_inc(sem("expo_t1"), 1)
                    need(dve, "att", f.n)
                    need(dve, "row_inv", f.n)
                    for k in range(blocks):
                        op = dve.scalar_tensor_tensor(out=z[2][:, k, :], in0=block_of(F[0], k),
                                                      scalar=row_inv[:, k:k + 1], in1=x2[:, k, :],
                                                      op0=ALU.mult, op1=ALU.add)
                    op.then_inc(sem("z2"), 1)
                    need(dve, "z2", f.n)
                    statistics(2, lambda i: z[2][:, i, :], f)
                if b is not None:
                    need(dve, "tr", b.n)
                    dve.tensor_scalar(reset[:, :], tr[:, :], 0.5, 0.5, ALU.mult, ALU.add)\
                        .then_inc(sem("reset"), 1)
                    need(dve, "reset", b.n)
                    dve.scalar_tensor_tensor(out=gated[:, :], in0=B[1][:, :], scalar=vcol("hh_n"),
                                             in1=reset[:, :], op0=ALU.add, op1=ALU.mult)\
                        .then_inc(sem("gated"), 1)
                    need(dve, "gin_ps", b.n)
                    need(dve, "gated", b.n)
                    dve.tensor_tensor(new_pre[:, :], B[0][:, :], gated[:, :], ALU.add)\
                        .then_inc(sem("new_pre"), 1)
                if f is not None:
                    normalize(2, x3, lambda i: z[2][:, i, :], f, "x3")
                if b is not None:
                    need(dve, "x_less_new", b.n)
                    need(dve, "tz", b.n)
                    dve.scalar_tensor_tensor(out=mixed[:, :], in0=tz[:, :], scalar=1.0, in1=x_less_new[:, :],
                                             op0=ALU.add, op1=ALU.mult).then_inc(sem("mixed"), 1)
                    need(dve, "x_plus_new", b.n)
                    need(dve, "mixed", b.n)
                    dve.scalar_tensor_tensor(out=y3t[:, :], in0=mixed[:, :], scalar=0.5,
                                             in1=x_plus_new[:, :], op0=ALU.mult, op1=ALU.add)\
                        .then_inc(sem("y3t"), 1)
                    need(dve, "y3_ps", b.n)
                    statistics(3, lambda i: block_of(B[1], i), b)
                    need(dve, "stored", b.prev_dma)
                    normalize(3, out_sb, lambda i: block_of(B[1], i), b, "out_rows")

            over_pairs(dve, steps)

        @block.tensor
        def _(pe):
            pe.wait_ge(sem("params"), 16 * 6)
            pe.wait_ge(sem("pool_init"), 4)
            pe.wait_ge(sem("self_diag"), 1)
            pe.wait_ge(sem("bias_parts"), 1)
            pe.wait_ge(sem("w_parts"), 1)

            def add_bias(bank, name):
                n = BIAS_ROWS.index(name)
                pe.matmul(bank[:, :].rearrange("p (k c) -> p k c", k=blocks), ones_rows[:, :], bias_parts[:, n:n + 1, :].broadcast_to([FEATS, blocks, P]),
                          start=True, stop=False, skip_group_check=True)

            def split(bank, w_at, high, low, start, stop):
                for n, (w, part) in enumerate(((w_hi, high), (w_hi, low), (w_lo, high))):
                    op = pe.matmul(bank, block_of(w, w_at), part, start=start and n == 0, stop=stop and n == 2)
                return op

            def transposes(bank, src):
                for k in range(blocks):
                    op = pe.transpose(block_of(bank, k), src[:, k, :], ident[:, :])
                return op

            def weigh_nodes(bank, rows, weights, diag=None):
                for g in range(2):
                    for t in range(tiles):
                        op = pe.matmul(bank[:, g * nodes:(g + 1) * nodes], rows[:, tiles * g + t, :],
                                       weights[:, tiles * g + t, :], start=(t == 0),
                                       stop=(t == tiles - 1 and diag is None), skip_group_check=True)
                    if diag is not None:
                        for t in range(tiles):
                            op = pe.matmul(block_of(bank, tiles * g + t), rows[:, tiles * g + t, :],
                                           diag[:, :], start=False, stop=True, skip_group_check=True)
                return op

            conv = [(tap, n) for tap in range(taps) for n in range(3)]

            def conv2(lo, hi):
                for at in range(lo, hi):
                    tap, n = conv[at]
                    w, part = ((w_hi, hch), (w_hi, hcl), (w_lo, hch))[n]
                    op = pe.matmul(B[0][:, :].rearrange("p (g n) -> p g n", g=2), block_of(w, C2 + tap),
                                   part[:, :, tap:tap + nodes], start=(at == 0), stop=(at == len(conv) - 1))
                return op

            def steps(f, b):
                if f is not None:
                    need(pe, "x_in", f.dma)
                    need(pe, "adjt_in", f.dma)
                    need(pe, "expo_t0", f.prev)
                    weigh_nodes(F[2], x_in, adjt_in).then_inc(sem("u0_ps"), 1)
                if b is not None:
                    need(pe, "x3", b.n)
                    need(pe, "out_rows", b.prev)
                    transposes(B[1], x3).then_inc(sem("x3t_ps"), 1)
                if f is not None:
                    need(pe, "u0", f.n)
                    need(pe, "expo_t1", f.prev)
                    add_bias(F[3], "b0")
                    for k in range(blocks):
                        op = pe.matmul(block_of(F[3], k), block_of(u0, k), w0_sb[:, :], start=False,
                                       stop=True, skip_group_check=True)
                    op.then_inc(sem("y0"), 1)
                if b is not None:
                    need(pe, "x3_parts", b.n)
                    need(pe, "tr", b.prev)
                    split(B[2][:, :], C1, x3h[:, :], x3l[:, :], True, True).then_inc(sem("conv1"), 1)
                    need(pe, "tz", b.prev)
                    split(B[3][:, :], SE, x3h[:, :], x3l[:, :], True, True).then_inc(sem("s_ps"), 1)
                    add_bias(B[1], "b_msg")
                    for k in range(blocks):
                        op = pe.matmul(block_of(B[1], k), block_of(x3t, k), wmsg_sb[:, :], start=False,
                                       stop=True, skip_group_check=True)
                    op.then_inc(sem("msg_ps"), 1)
                    need(pe, "feat_l", b.n)
                    need(pe, "feat_sq", b.n)
                    need(pe, "feat_r", b.n)
                    need(pe, "hc", b.n)
                    for g in range(2):
                        for t in range(tiles):
                            op = pe.matmul(B[2 + g][:, t * nodes:(t + 1) * nodes],
                                           feat_l[:, (tiles * g + t) * P:(tiles * g + t + 1) * P],
                                           feat_r[:, g * nodes:(g + 1) * nodes], start=True, stop=True,
                                           skip_group_check=True)
                    op.then_inc(sem("dist"), 1)
                    need(pe, "hc_parts", b.n)
                    need(pe, "new_pre", b.prev)
                    conv2(0, 9)
                if f is not None:
                    need(pe, "x1", f.n)
                    weigh_nodes(F[2], x1, adjt_in, self_diag).then_inc(sem("u1_ps"), 1)
                if b is not None:
                    need(pe, "msg", b.n)
                    need(pe, "adj_near", b.n)
                    weigh_nodes(B[1], msg, adj_near).then_inc(sem("nmp"), 1)
                if f is not None:
                    need(pe, "u1c", f.n)
                    for j in range(2):
                        op = pe.matmul(F[j][:, :], block_of(w1_sb, j), u1[:, :], start=True, stop=True)
                        op.then_inc(sem(f"h1_ps{j}"), 1)
                if b is not None:
                    conv2(9, 18)
                if f is not None:
                    need(pe, "h1_0", f.n)
                    need(pe, "h1_1", f.n)
                    add_bias(F[3], "b2")
                    for k in range(blocks):
                        for j in range(2):
                            op = pe.matmul(block_of(F[3], k), h1[:, j, k * P:(k + 1) * P], w2_sb[:, j, :],
                                           start=False, stop=(j == 1), skip_group_check=True)
                    op.then_inc(sem("y1"), 1)
                if b is not None:
                    conv2(18, 39)
                if f is not None:
                    need(pe, "x2", f.n)
                    transposes(F[2], x2).then_inc(sem("x2t_ps"), 1)
                if b is not None:
                    conv2(39, 45)
                if f is not None:
                    need(pe, "x2t", f.n)
                    pe.matmul(F[3][:, :], watt_sb[:, :], x2t[:, :], start=True, stop=True)\
                        .then_inc(sem("q_ps"), 1)
                if b is not None:
                    conv2(45, 51).then_inc(sem("conv2"), 1)
                if f is not None:
                    need(pe, "q", f.n)
                    need(pe, "mask_neg", f.n)
                    for g in range(2):
                        pe.matmul(F[g][:, :].rearrange("p (t n) -> p t n", t=tiles), first_row[:, :],
                                  mask_neg[:, g:g + 1, :].broadcast_to([P, tiles, nodes]), start=True, stop=False,
                                  skip_group_check=True)
                        for t in range(tiles):
                            op = pe.matmul(F[g][:, t * nodes:(t + 1) * nodes], block_of(q, tiles * g + t),
                                           x2t[:, g * nodes:(g + 1) * nodes], start=False, stop=True,
                                           skip_group_check=True)
                    op.then_inc(sem("scores"), 1)
                if b is not None:
                    need(pe, "nm_parts", b.n)
                    split(B[1][:, :], HH + 2, x3h[:, :], x3l[:, :], True, True)
                    for gate in range(2):
                        bank = B[2 + gate][:, :]
                        split(bank, HH + gate, x3h[:, :], x3l[:, :], True, False)
                        split(bank, IH + 3 + gate, nmh[:, :], nml[:, :], False, False)
                if f is not None:
                    need(pe, "expo", f.n)
                    for g in range(2):
                        for t in range(tiles):
                            for s in range(tiles):
                                at = t * nodes + s * P
                                op = pe.transpose(F[2 + g][:, at:at + P],
                                                  expo[:, tiles * g + s, t * P:(t + 1) * P], ident[:, :])
                    op.then_inc(sem("expo_t_ps"), 1)
                if b is not None:
                    need(pe, "xc_parts", b.n)
                    for gate in range(2):
                        op = split(B[2 + gate][:, :], IH + gate, xch[:, :], xcl[:, :], False, True)
                    op.then_inc(sem("gates_ps"), 1)
                    split(B[0][:, :], IH + 2, xch[:, :], xcl[:, :], True, False)
                    split(B[0][:, :], IH + 5, nmh[:, :], nml[:, :], False, True).then_inc(sem("gin_ps"), 1)
                if f is not None:
                    need(pe, "expo_t0", f.n)
                    need(pe, "expo_t1", f.n)
                    for g in range(2):
                        for s in range(tiles):
                            for t in range(tiles):
                                op = pe.matmul(block_of(F[0], tiles * g + s),
                                               expo_t[:, tiles * g + t, s * P:(s + 1) * P],
                                               x2[:, tiles * g + t, :], start=(t == 0),
                                               stop=(t == tiles - 1), skip_group_check=True)
                    op.then_inc(sem("att"), 1)
                if b is not None:
                    need(pe, "y3t", b.n)
                    for k in range(blocks):
                        op = pe.transpose(block_of(B[1], k), block_of(y3t, k), ident[:, :])
                    op.then_inc(sem("y3_ps"), 1)

            over_pairs(pe, steps)


def kernel(**inputs):
    import numpy as np
    import concourse.bacc as bacc
    from concourse import mybir as _mybir
    from concourse.bass_utils import run_bass_kernel_spmd as run

    a = {n: np.asarray(v) for n, v in inputs.items()}
    ch = a["x"].shape[-1]
    f32 = np.float32

    def spread(v, starts=(S_ROWS, SQ_ROWS, ONE_ROWS)):
        to = np.zeros((P,) + v.shape[1:], f32)
        for s in starts:
            to[s:s + v.shape[0]] = v
        return to

    columns = {
        "prelu_a": np.broadcast_to(a["L0_gnn_prelu_a"].reshape(1), (ch,)),
        "eps": np.broadcast_to(a["L1_gnn_eps"], (ch,)),
        "b1_lo": a["L1_gnn_b1"][:ch], "b1_hi": a["L1_gnn_b1"][ch:],
        "b_se": spread(a["L3_gnn_b_se"]),
        **{f"bn{n}_{k}": a[f"L3_gnn_bn{n}_{k}"] for n in (1, 2) for k in "gbmv"},
        **{f"{w}_{g}": a[f"L3_gnn_b_{w}"][i * ch:(i + 1) * ch] for w in ("ih", "hh") for i, g in enumerate("rzn")},
    }
    w_ih = a["L3_gnn_w_ih"].reshape(3, ch, 2, ch).transpose(3, 2, 0, 1).reshape(ch, 6, ch)
    w_hh = a["L3_gnn_w_hh"].reshape(3, ch, ch).transpose(2, 0, 1)
    arrays = {
        "x": a["x"], "adj": a["adj"], "adj_t": a["adj"].transpose(0, 2, 1), "mask": a["nodemask"],
        "vecs": np.stack([columns[n] for n in VEC], axis=1),
        "bias_rows": np.stack([a["L0_gnn_bias"], a["L1_gnn_b2"], a["L3_gnn_b_msg"]]),
        "w0": a["L0_gnn_W"], "w1": a["L1_gnn_W1"], "w2": a["L1_gnn_W2"], "w_att": a["L2_gnn_W"],
        "w_se": spread(a["L3_gnn_w_se"]).T, "w_conv1": a["L3_gnn_conv1_w"][:, :, 0].T,
        "w_conv2": a["L3_gnn_conv2_w"].transpose(1, 2, 0), "w_msg": a["L3_gnn_w_msg"].T,
        "w_ih": w_ih, "w_hh": w_hh,
    }
    nc = bacc.Bacc("TRN2", target_bir_lowering=False, num_devices=1)
    feeds, aps = {}, []
    for name, v in arrays.items():
        v = np.ascontiguousarray(v)
        feeds[f"in_{name}"] = v
        aps.append(nc.dram_tensor(f"in_{name}", v.shape, _mybir.dt.from_np(v.dtype), kind="ExternalInput").ap())
    aps.append(nc.dram_tensor("out_x", a["x"].shape, _mybir.dt.float32, kind="ExternalOutput").ap())
    adjacency_block_kernel(nc, *aps)
    return run(nc, [feeds], core_ids=[0]).results[0]["out_x"]
```

```python
from contextlib import ExitStack

import concourse.bass as bass
from concourse import mybir
from concourse.alu_op_type import AluOpType as ALU

ACT = mybir.ActivationFunctionType
F32 = mybir.dt.float32
F32R = mybir.dt.float32r
BF16 = mybir.dt.bfloat16
I32 = mybir.dt.int32

P = 128
EPS = 1e-5
MASKED = -1e30
LOWEST = -3.0e38

VEC = ["prelu_a", "eps", "b1_lo", "b1_hi", "b_se", "bn1_g", "bn1_b", "bn1_m", "bn1_v",
       "bn2_g", "bn2_b", "bn2_m", "bn2_v", "ih_r", "ih_z", "ih_n", "hh_r", "hh_z", "hh_n"]
V = {name: i for i, name in enumerate(VEC)}
BIAS_ROWS = ["b0", "b2", "b_msg"]
S_ROWS, SQ_ROWS, ONE_ROWS, FEATS = 0, 32, 64, 96


def adjacency_block_kernel(nc, x, adj, adj_t, mask, vecs, bias_rows, w0, w1, w2, w_att, w_se, w_conv1,
                           w_conv2, w_msg, w_ih, w_hh, out):
    graphs, nodes, ch = x.shape
    pairs = graphs // 2
    blocks = 2 * nodes // P
    tiles = nodes // P
    cols = 2 * nodes
    taps = w_conv2.shape[1]
    pad = taps // 2
    assert ch == P and blocks == 4 and cols == 512

    x_d = x.rearrange("(k g) (t p) c -> k p (g t) c", g=2, p=P)
    adj_d = adj.rearrange("(k g) (t p) m -> k p (g t) m", g=2, p=P)
    adj_t_d = adj_t.rearrange("(k g) (t p) n -> k p (g t) n", g=2, p=P)
    mask_d = mask.rearrange("(k o g) n -> k o (g n)", g=2, o=1)
    out_d = out.rearrange("(k g) (t p) c -> k p (g t) c", g=2, p=P)

    with ExitStack() as ctx:
        def sb(name, shape, dt=F32):
            return ctx.enter_context(nc.sbuf_tensor(name, shape, dt))

        sems = {}

        def sem(name):
            if name not in sems:
                sems[name] = ctx.enter_context(nc.semaphore(name))
            return sems[name]

        def need(eng, name, count):
            if isinstance(count, int) and count <= 0:
                return
            eng.wait_ge(sem(name), count)

        def need_apart(eng, name, count):
            eng.wait_ge(sem("params"), 16)
            need(eng, name, count)

        class Pair:
            def __init__(self, eng, n):
                held = (lambda v: eng.snap(eng.to_reg(v))) if not isinstance(n, int) else (lambda v: v)
                self.n, self.prev = held(n), held(n - 1)
                self.dma, self.prev_dma = held(n * 16), held(n * 16 - 16)

        def do(step, pair):
            if pair is not None:
                step(pair)

        def over_pairs(eng, steps):
            def stages(f):
                steps(*(Pair(eng, f - k) if 1 <= f - k <= pairs else None for k in range(4)))

            for f in range(1, 5):
                stages(f)
            with eng.Fori(5, pairs + 1) as f:
                steps(*(Pair(eng, f - k) for k in range(4)))
            for f in range(pairs + 1, pairs + 4):
                stages(f)

        vec = sb("vec", [P, len(VEC)])
        w0_sb = sb("w0_sb", [P, P])
        w1_sb = sb("w1_sb", [P, 2 * P])
        w2_sb = sb("w2_sb", [P, 2, P])
        watt_sb = sb("watt_sb", [P, P])
        wmsg_sb = sb("wmsg_sb", [P, P])
        n_split = P * (1 + 1 + taps + 9)
        w_raw = sb("w_raw", [P, n_split])
        w_hi = sb("w_hi", [P, n_split], F32R)
        w_lo = sb("w_lo", [P, n_split], F32R)
        bias_raw = sb("bias_raw", [FEATS, 3, P])
        bias_rest = sb("bias_rest", [FEATS, 3, P])
        bias_hi = sb("bias_hi", [FEATS, 3, P], BF16)
        bias_mid = sb("bias_mid", [FEATS, 3, P], BF16)
        bias_parts = sb("bias_parts", [FEATS, 3, P], BF16)
        ident = sb("ident", [P, P])
        self_diag = sb("self_diag", [P, P])
        ones_rows = sb("ones_rows", [FEATS, P], BF16)
        first_row = sb("first_row", [P, P], BF16)
        bn1_scale = sb("bn1_scale", [P, 1])
        bn1_shift = sb("bn1_shift", [P, 1])
        bn2_scale = sb("bn2_scale", [P, 1])
        bn2_shift = sb("bn2_shift", [P, 1])
        bn_tmp = sb("bn_tmp", [P, 4])
        minus_half = sb("minus_half", [P, 4])
        one_minus_a = sb("one_minus_a", [P, 1])
        half_br = sb("half_br", [P, 1])
        half_bz = sb("half_bz", [P, 1])

        x_in = sb("x_in", [P, blocks, P])
        adj_in = sb("adj_in", [P, blocks, nodes])
        adjt_in = sb("adjt_in", [P, blocks, nodes])
        mask_in = sb("mask_in", [P, cols], I32)
        unmasked = sb("unmasked", [P, 2, nodes])
        masked = sb("masked", [P, 2, nodes])
        mask_neg = sb("mask_neg", [P, 2, nodes], BF16)
        adj_m = sb("adj_m", [P, blocks, nodes])
        u0 = sb("u0", [P, cols])
        u1 = sb("u1", [P, cols])
        neg0 = sb("neg0", [P, cols])
        z = [sb(f"z{n}", [P, blocks, P]) for n in range(3)]
        res0 = sb("res0", [P, cols])
        x1 = sb("x1", [P, blocks, P])
        x2 = sb("x2", [P, blocks, P])
        x3 = sb("x3", [P, blocks, P])
        h1 = sb("h1", [P, 2, cols])
        x2t = sb("x2t", [P, cols])
        q = sb("q", [P, cols])
        prob = sb("prob", [P, blocks, nodes])
        expo = sb("expo", [P, blocks, nodes])
        expo_t = sb("expo_t", [P, blocks, nodes])
        row_max = sb("row_max", [P, blocks])
        minus_max = sb("minus_max", [P, blocks])
        row_sum = sb("row_sum", [P, blocks])
        row_inv = sb("row_inv", [P, blocks])
        bn6 = sb("bn6", [P, 4, blocks, 6])
        stats = sb("stats", [P, 4, blocks, 2])
        var_eps = sb("var_eps", [P, 4, blocks])
        rstd = sb("rstd", [P, 4, blocks])
        adjt_kept = sb("adjt_kept", [P, blocks, nodes])
        x3t = sb("x3t", [P, cols])
        x3h = sb("x3h", [P, cols], F32R)
        x3l = sb("x3l", [P, cols], F32R)
        hc = sb("hc", [P, 2, nodes])
        hch = sb("hch", [P, 2, nodes + 2 * pad], F32R)
        hcl = sb("hcl", [P, 2, nodes + 2 * pad], F32R)
        feat_r = sb("feat_r", [FEATS, cols])
        feat_l = sb("feat_l", [FEATS, cols])
        msg = sb("msg", [P, blocks, P])
        near = sb("near", [P, blocks, nodes])
        adj_near = sb("adj_near", [P, blocks, nodes])
        nmh = sb("nmh", [P, cols], F32R)
        nml = sb("nml", [P, cols], F32R)
        xc_pre = sb("xc_pre", [P, cols])
        xc = sb("xc", [P, cols])
        xch = sb("xch", [P, cols], F32R)
        xcl = sb("xcl", [P, cols], F32R)
        tr = sb("tr", [P, cols])
        tz = sb("tz", [P, cols])
        reset = sb("reset", [P, cols])
        gated = sb("gated", [P, cols])
        new_pre = sb("new_pre", [P, cols])
        new = sb("new", [P, cols])
        x_less_new = sb("x_less_new", [P, cols])
        x_plus_new = sb("x_plus_new", [P, cols])
        mixed = sb("mixed", [P, cols])
        y3t = sb("y3t", [P, cols])
        out_sb = sb("out_sb", [P, blocks, P])

        F = [ctx.enter_context(nc.psum_tensor(f"front{n}", [P, 512], F32)) for n in range(4)]
        B = [ctx.enter_context(nc.psum_tensor(f"back{n}", [P, 512], F32)) for n in range(4)]

        def block_of(t, k):
            return t[:, k * P:(k + 1) * P]

        def vcol(name):
            return vec[:, V[name]:V[name] + 1]

        SE, C1, C2, IH, HH = 0, 1, 2, 2 + taps, 2 + taps + 6

        block = ctx.enter_context(nc.Block())

        @block.sync
        def _(sp):
            sp.dma_start(vec[:, :], vecs).then_inc(sem("params"), 16)
            for dst, src in ((w0_sb[:, :], w0), (w1_sb[:, :], w1), (watt_sb[:, :], w_att),
                             (wmsg_sb[:, :], w_msg),
                             (w2_sb[:, :, :], w2.rearrange("(j p) c -> p j c", p=P))):
                sp.dma_start(dst, src).then_inc(sem("params"), 16)
            for row in (0, 32, 64):
                sp.dma_start(bias_raw[row:row + 1, :, :],
                             bias_rows.rearrange("(o r) c -> o r c", o=1)).then_inc(sem("bias_in"), 16)
            for at, src, count in ((SE, w_se, 1), (C1, w_conv1, 1), (C2, w_conv2, taps),
                                   (IH, w_ih, 6), (HH, w_hh, 3)):
                dst = w_raw[:, at * P:(at + count) * P]
                if count > 1:
                    dst = dst.rearrange("p (k c) -> p k c", k=count)
                sp.dma_start(dst, src).then_inc(sem("weights_in"), 16)

            def load_x(f):
                need(sp, "res0", f.prev)
                sp.dma_start(x_in[:, :, :], x_d[f.prev]).then_inc(sem("x_in"), 16)

            def load_adjt(f):
                need(sp, "u1_ps", f.prev)
                sp.dma_start(adjt_in[:, :, :], adj_t_d[f.prev]).then_inc(sem("adjt_in"), 16)

            def load_mask_and_adj(f):
                need(sp, "adj_m", f.prev)
                sp.dma_start(mask_in[:, :], mask_d[f.prev].broadcast_to([P, cols])).then_inc(sem("mask_in"), 16)
                sp.dma_start(adj_in[:, :, :], adj_d[f.prev]).then_inc(sem("adj_in"), 16)

            def load_adjt_kept(s):
                need(sp, "adj_near", s.prev)
                sp.dma_start(adjt_kept[:, :, :], adj_t_d[s.prev]).then_inc(sem("adjt_kept"), 16)

            def store(d):
                need(sp, "out_rows", d.n)
                sp.dma_start(out_d[d.prev], out_sb[:, :, :]).then_inc(sem("stored"), 16)

            def steps(f, s, c, d):
                do(load_adjt, f)
                do(load_x, f)
                do(load_mask_and_adj, f)
                do(store, d)
                do(load_adjt_kept, s)

            over_pairs(sp, steps)
            sp.wait_ge(sem("stored"), 16 * pairs)

        @block.gpsimd
        def _(pool):
            pool.memset(ident[:, :], 0.0).then_inc(sem("pool_init"), 1)
            pool.memset(minus_half[:, :], -0.5)
            pool.memset(ones_rows[:, :], 1.0)
            pool.memset(first_row[:, :], 0.0)
            pool.memset(feat_l[:, :], 1.0)
            pool.memset(feat_r[:, :], 1.0)
            pool.memset(hch[:, :, :].bitcast(F32), 0.0)
            pool.memset(hcl[:, :, :].bitcast(F32), 0.0).then_inc(sem("pool_init"), 1)
            pool.wait_ge(sem("pool_init"), 2)
            pool.memset(first_row[0:1, :], 1.0).then_inc(sem("pool_init"), 1)
            pool.affine_select(out=ident[:, :], in_=ident[:, :], compare_op=ALU.not_equal, fill=1.0,
                               base=0, pattern=[[-1, P]], channel_multiplier=1).then_inc(sem("pool_init"), 1)
            pool.wait_ge(sem("bn_var"), 1)
            pool.tensor_tensor(bn_tmp[:, 2:4], bn_tmp[:, 0:2], minus_half[:, 0:2], ALU.pow)\
                .then_inc(sem("bn_rstd"), 1)

            def masks(f):
                need_apart(pool, "mask_in", f.dma)
                need(pool, "soft_in", f.prev)
                pool.tensor_scalar(masked[:, :, :], mask_in[:, :].rearrange("p (g n) -> p g n", g=2),
                                   0.0, None, ALU.is_equal).then_inc(sem("masked"), 1)
                need_apart(pool, "masked", f.n)
                pool.tensor_scalar(unmasked[:, :, :], masked[:, :, :], -1.0, 1.0, ALU.mult, ALU.add)
                pool.tensor_scalar(mask_neg[:, :, :], masked[:, :, :], MASKED, None, ALU.mult)\
                    .then_inc(sem("mask_neg"), 1)
                need(pool, "mask_neg", f.n)
                need(pool, "adj_in", f.dma)
                for g in range(2):
                    at = slice(tiles * g, tiles * (g + 1))
                    keep = unmasked[:, g:g + 1, :].broadcast_to([P, tiles, nodes])
                    op = pool.tensor_tensor(adj_m[:, at, :], adj_in[:, at, :], keep, ALU.mult)
                op.then_inc(sem("adj_keep"), 1)
                need(pool, "adj_keep", f.n)
                for g in range(2):
                    at = slice(tiles * g, tiles * (g + 1))
                    fill = masked[:, g:g + 1, :].broadcast_to([P, tiles, nodes])
                    op = pool.tensor_tensor(adj_m[:, at, :], adj_m[:, at, :], fill, ALU.add)
                op.then_inc(sem("adj_m"), 1)

            def rsqrt(n):
                def step(k):
                    need(pool, f"var{n}", k.n)
                    pool.tensor_tensor(rstd[:, n, :], var_eps[:, n, :], minus_half[:, 0:blocks], ALU.pow)\
                        .then_inc(sem(f"rstd{n}"), 1)
                return step

            def minus_two_s(c):
                need_apart(pool, "feat_s", c.n)
                need(pool, "dist", c.prev)
                pool.tensor_scalar(feat_l[0:32, :], feat_r[0:32, :], -2.0, None, ALU.mult)\
                    .then_inc(sem("feat_l"), 1)

            def around_new(c):
                need(pool, "new", c.n)
                pool.tensor_tensor(x_less_new[:, :], x3t[:, :], new[:, :], ALU.subtract)\
                    .then_inc(sem("x_less_new"), 1)
                pool.tensor_tensor(x_plus_new[:, :], x3t[:, :], new[:, :], ALU.add)\
                    .then_inc(sem("x_plus_new"), 1)

            def steps(f, s, c, d):
                do(rsqrt(1), s)
                do(rsqrt(3), d)
                do(minus_two_s, c)
                do(rsqrt(0), f)
                do(rsqrt(2), s)
                do(masks, f)
                do(around_new, c)

            over_pairs(pool, steps)

        @block.scalar
        def _(act):
            act.wait_ge(sem("gate_bias"), 1)

            def copy_x3t(c):
                need(act, "x3t_ps", c.n)
                need(act, "x_plus_new", c.prev)
                act.activation(x3t[:, :], B[1][:, :], ACT.Copy).then_inc(sem("x3t"), 1)

            def copy_u0(f):
                need(act, "u0_ps", f.n)
                act.activation(u0[:, :], F[2][:, :], ACT.Copy).then_inc(sem("u0"), 1)

            def hidden_conv(c):
                need(act, "conv1", c.n)
                act.activation(hc[:, :, :], B[2][:, :].rearrange("p (g n) -> p g n", g=2), ACT.Relu,
                               bias=bn1_shift[:, :], scale=bn1_scale[:, :]).then_inc(sem("hc"), 1)

            def minus_part(f):
                need(act, "y0", f.n)
                act.activation(neg0[:, :], F[3][:, :], ACT.Relu, scale=-1.0).then_inc(sem("neg0"), 1)

            def features(c):
                need(act, "s_ps", c.n)
                act.activation(feat_r[0:64, :], B[3][0:64, :], ACT.Identity,
                               bias=vec[0:64, V["b_se"]:V["b_se"] + 1]).then_inc(sem("feat_s"), 1)
                act.activation(feat_l[64:96, :], B[3][64:96, :], ACT.Square,
                               bias=vec[64:96, V["b_se"]:V["b_se"] + 1]).then_inc(sem("feat_sq"), 1)

            def relu_msg(c):
                need(act, "msg_ps", c.n)
                act.activation(msg[:, :, :], B[1][:, :].rearrange("p (k c) -> p k c", k=blocks),
                               ACT.Relu).then_inc(sem("msg"), 1)

            def nearness(c):
                need(act, "dist", c.n)
                for g in range(2):
                    act.activation(near[:, tiles * g:tiles * (g + 1), :],
                                   B[2 + g][:, :].rearrange("p (t n) -> p t n", t=tiles),
                                   ACT.Exp, scale=-1.0).then_inc(sem(f"near{g}"), 1)

            def copy_u1(f):
                need(act, "u1_ps", f.n)
                act.activation(u1[:, :], F[2][:, :], ACT.Copy).then_inc(sem("u1c"), 1)

            def high_nm(c):
                need(act, "nmp", c.n)
                act.activation(nmh[:, :], B[1][:, :], ACT.Copy).then_inc(sem("nm_high"), 1)

            def hidden_gin(f):
                for j in range(2):
                    need(act, f"h1_ps{j}", f.n)
                    act.activation(h1[:, j, :], F[j][:, :], ACT.Relu,
                                   bias=vcol("b1_lo" if j == 0 else "b1_hi")).then_inc(sem(f"h1_{j}"), 1)

            def copy_x2t(s):
                need(act, "x2t_ps", s.n)
                act.activation(x2t[:, :], F[2][:, :], ACT.Copy).then_inc(sem("x2t"), 1)

            def copy_q(s):
                need(act, "q_ps", s.n)
                act.activation(q[:, :], F[2][:, :], ACT.Copy).then_inc(sem("q"), 1)

            def relu_xc(c):
                need(act, "xc_pre", c.n)
                act.activation(xc[:, :], xc_pre[:, :], ACT.Relu, bias=bn2_shift[:, :])\
                    .then_inc(sem("xc"), 1)

            def exponentials(s):
                need(act, "soft_in", s.n)
                for k in range(blocks):
                    op = act.activation(expo[:, k, :], prob[:, k, :], ACT.Exp,
                                        bias=minus_max[:, k:k + 1], accum_out=row_sum[:, k:k + 1])
                op.then_inc(sem("expo"), 1)

            def copy_expo_t0(s):
                need(act, "expo_t_ps", s.n)
                act.activation(expo_t[:, 0:2, :], F[2][:, :].rearrange("p (t n) -> p t n", t=tiles),
                               ACT.Copy).then_inc(sem("expo_t0"), 1)

            def gates(c):
                need(act, "gates_ps", c.n)
                act.activation(tr[:, :], B[2][:, :], ACT.Tanh, bias=half_br[:, :], scale=0.5)\
                    .then_inc(sem("tr"), 1)
                act.activation(tz[:, :], B[3][:, :], ACT.Tanh, bias=half_bz[:, :], scale=0.5)\
                    .then_inc(sem("tz"), 1)

            def new_state(c):
                need(act, "new_pre", c.n)
                act.activation(new[:, :], new_pre[:, :], ACT.Tanh, bias=vcol("ih_n"))\
                    .then_inc(sem("new"), 1)

            def steps(f, s, c, d):
                do(copy_x3t, c)
                do(copy_u0, f)
                do(hidden_conv, c)
                do(features, c)
                do(minus_part, f)
                do(relu_msg, c)
                do(nearness, c)
                do(copy_x2t, s)
                do(copy_q, s)
                do(exponentials, s)
                do(high_nm, c)
                do(copy_expo_t0, s)
                do(relu_xc, c)
                do(copy_u1, f)
                do(gates, c)
                do(new_state, c)
                do(hidden_gin, f)

            over_pairs(act, steps)

        @block.vector
        def _(dve):
            dve.wait_ge(sem("params"), 16 * 6)
            for n, name in enumerate(("bn1_v", "bn2_v")):
                op = dve.tensor_scalar(bn_tmp[:, n:n + 1], vcol(name), EPS, None, ALU.add)
            op.then_inc(sem("bn_var"), 1)
            dve.tensor_scalar(one_minus_a[:, :], vcol("prelu_a"), -1.0, 1.0, ALU.mult, ALU.add)
            dve.tensor_tensor(half_br[:, :], vcol("ih_r"), vcol("hh_r"), ALU.add)
            dve.tensor_tensor(half_bz[:, :], vcol("ih_z"), vcol("hh_z"), ALU.add).then_inc(sem("dve_init"), 1)
            dve.wait_ge(sem("dve_init"), 1)
            dve.tensor_scalar(half_br[:, :], half_br[:, :], 0.5, None, ALU.mult)
            dve.tensor_scalar(half_bz[:, :], half_bz[:, :], 0.5, None, ALU.mult).then_inc(sem("dve_init"), 1)
            dve.wait_ge(sem("bn_rstd"), 1)
            dve.tensor_tensor(bn1_scale[:, :], vcol("bn1_g"), bn_tmp[:, 2:3], ALU.mult)
            dve.tensor_tensor(bn2_scale[:, :], vcol("bn2_g"), bn_tmp[:, 3:4], ALU.mult).then_inc(sem("dve_init"), 1)
            dve.wait_ge(sem("dve_init"), 3)
            dve.tensor_tensor(bn1_shift[:, :], vcol("bn1_m"), bn1_scale[:, :], ALU.mult)
            dve.tensor_tensor(bn2_shift[:, :], vcol("bn2_m"), bn2_scale[:, :], ALU.mult).then_inc(sem("dve_init"), 1)
            dve.wait_ge(sem("dve_init"), 4)
            dve.tensor_tensor(bn1_shift[:, :], vcol("bn1_b"), bn1_shift[:, :], ALU.subtract)
            dve.tensor_tensor(bn2_shift[:, :], vcol("bn2_b"), bn2_shift[:, :], ALU.subtract)\
                .then_inc(sem("gate_bias"), 1)
            dve.wait_ge(sem("pool_init"), 4)
            dve.tensor_scalar(self_diag[:, :], ident[:, :], vcol("eps"), None, ALU.mult).then_inc(sem("dve_init"), 1)
            dve.wait_ge(sem("dve_init"), 5)
            dve.tensor_tensor(self_diag[:, :], self_diag[:, :], ident[:, :], ALU.add).then_inc(sem("self_diag"), 1)
            dve.memset(bias_parts[:, :, :], 0.0).then_inc(sem("dve_init"), 1)
            dve.wait_ge(sem("bias_in"), 16 * 3)
            for row in (0, 32, 64):
                op = dve.tensor_copy(bias_hi[row:row + 1, :, :], bias_raw[row:row + 1, :, :])
            op.then_inc(sem("dve_init"), 1)
            dve.wait_ge(sem("dve_init"), 7)
            dve.tensor_copy(bias_parts[0:1, :, :], bias_hi[0:1, :, :])
            for row in (32, 64):
                op = dve.tensor_tensor(bias_rest[row:row + 1, :, :], bias_raw[row:row + 1, :, :],
                                       bias_hi[row:row + 1, :, :], ALU.subtract)
            op.then_inc(sem("dve_init"), 1)
            dve.wait_ge(sem("dve_init"), 8)
            dve.tensor_copy(bias_parts[32:33, :, :], bias_rest[32:33, :, :])
            dve.tensor_copy(bias_mid[64:65, :, :], bias_rest[64:65, :, :]).then_inc(sem("dve_init"), 1)
            dve.wait_ge(sem("dve_init"), 9)
            dve.tensor_tensor(bias_parts[64:65, :, :], bias_rest[64:65, :, :], bias_mid[64:65, :, :],
                              ALU.subtract).then_inc(sem("bias_parts"), 1)
            dve.wait_ge(sem("weights_in"), 16 * 5)
            dve.tensor_copy(w_hi[:, :], w_raw[:, :]).then_inc(sem("w_high"), 1)
            dve.wait_ge(sem("w_high"), 1)
            dve.tensor_tensor(w_lo[:, :], w_raw[:, :], w_hi[:, :].bitcast(F32), ALU.subtract)\
                .then_inc(sem("w_parts"), 1)

            def flat(t):
                return t[:, :, :].rearrange("p k c -> p (k c)")

            def statistics(n, src, k):
                for i in range(blocks):
                    op = dve.bn_stats(bn6[:, n, i, :], src(i))
                op.then_inc(sem(f"bn6_{n}"), 1)
                need_apart(dve, f"bn6_{n}", k.n)
                for i in range(blocks):
                    op = dve.bn_aggr(stats[:, n, i, :], bn6[:, n, i, :])
                op.then_inc(sem(f"stats{n}"), 1)
                need(dve, f"stats{n}", k.n)
                dve.tensor_scalar(var_eps[:, n, :], stats[:, n, :, 1], EPS, None, ALU.add)\
                    .then_inc(sem(f"var{n}"), 1)

            def normalize(n, dst, src, k, name):
                need(dve, f"rstd{n}", k.n)
                for i in range(blocks):
                    op = dve.tensor_scalar(dst[:, i, :], src(i), stats[:, n, i, 0:1], rstd[:, n, i:i + 1],
                                           ALU.subtract, ALU.mult)
                op.then_inc(sem(name), 1)

            def split_x3(c):
                need(dve, "x3t", c.n)
                dve.tensor_copy(x3h[:, :], x3t[:, :]).then_inc(sem("x3_high"), 1)
                need(dve, "x3_high", c.n)
                dve.tensor_tensor(x3l[:, :], x3t[:, :], x3h[:, :].bitcast(F32), ALU.subtract)\
                    .then_inc(sem("x3_parts"), 1)

            def residual0(f):
                need(dve, "neg0", f.n)
                dve.scalar_tensor_tensor(out=res0[:, :], in0=neg0[:, :], scalar=one_minus_a[:, :],
                                         in1=flat(x_in), op0=ALU.mult, op1=ALU.add).then_inc(sem("res0"), 1)
                need(dve, "res0", f.n)
                dve.tensor_tensor(flat(z[0]), F[3][:, :], res0[:, :], ALU.add).then_inc(sem("z0"), 1)
                need(dve, "z0", f.n)
                statistics(0, lambda i: z[0][:, i, :], f)

            def norm0(f):
                normalize(0, x1, lambda i: z[0][:, i, :], f, "x1")

            def residual1(s):
                need(dve, "y1", s.n)
                dve.tensor_tensor(flat(z[1]), F[3][:, :], flat(x1), ALU.add).then_inc(sem("z1"), 1)
                need(dve, "z1", s.n)
                statistics(1, lambda i: z[1][:, i, :], s)

            def norm1(s):
                normalize(1, x2, lambda i: z[1][:, i, :], s, "x2")

            def split_hc(c):
                need(dve, "hc", c.n)
                dve.tensor_copy(hch[:, :, pad:pad + nodes], hc[:, :, :]).then_inc(sem("hc_high"), 1)
                need(dve, "hc_high", c.n)
                dve.tensor_tensor(hcl[:, :, pad:pad + nodes], hc[:, :, :],
                                  hch[:, :, pad:pad + nodes].bitcast(F32), ALU.subtract)\
                    .then_inc(sem("hc_parts"), 1)

            def square_s(c):
                need(dve, "feat_s", c.n)
                dve.tensor_tensor(feat_r[32:64, :], feat_r[32:64, :], feat_r[32:64, :], ALU.mult)\
                    .then_inc(sem("feat_r"), 1)

            def weigh_adj(c):
                need(dve, "adjt_kept", c.dma)
                for g in range(2):
                    need(dve, f"near{g}", c.n)
                    at = slice(tiles * g, tiles * (g + 1))
                    op = dve.tensor_tensor(adj_near[:, at, :], near[:, at, :], adjt_kept[:, at, :],
                                           ALU.mult)
                op.then_inc(sem("adj_near"), 1)

            def low_nm(c):
                need(dve, "nm_high", c.n)
                dve.tensor_tensor(nml[:, :], B[1][:, :], nmh[:, :].bitcast(F32), ALU.subtract)\
                    .then_inc(sem("nm_parts"), 1)

            def pre_xc(c):
                need(dve, "conv2", c.n)
                dve.scalar_tensor_tensor(out=xc_pre[:, :], in0=B[0][:, :], scalar=bn2_scale[:, :],
                                         in1=x3t[:, :], op0=ALU.mult, op1=ALU.add)\
                    .then_inc(sem("xc_pre"), 1)

            def split_xc(c):
                need(dve, "xc", c.n)
                dve.tensor_copy(xch[:, :], xc[:, :]).then_inc(sem("xc_high"), 1)
                need(dve, "xc_high", c.n)
                dve.tensor_tensor(xcl[:, :], xc[:, :], xch[:, :].bitcast(F32), ALU.subtract)\
                    .then_inc(sem("xc_parts"), 1)

            def weigh_scores(s):
                need_apart(dve, "scores", s.n)
                need(dve, "adj_m", s.n)
                for k in range(blocks):
                    g, t = divmod(k, tiles)
                    op = dve.tensor_tensor_reduce(out=prob[:, k, :], in0=F[g][:, t * nodes:(t + 1) * nodes],
                                                  in1=adj_m[:, k, :], scale=1.0, scalar=LOWEST,
                                                  op0=ALU.mult, op1=ALU.max,
                                                  accum_out=row_max[:, k:k + 1])
                op.then_inc(sem("prob"), 1)
                need(dve, "prob", s.n)
                dve.tensor_scalar(minus_max[:, :], row_max[:, :], -1.0, None, ALU.mult)\
                    .then_inc(sem("soft_in"), 1)

            def invert_sums(s):
                need(dve, "expo", s.n)
                dve.reciprocal(row_inv[:, :], row_sum[:, :]).then_inc(sem("row_inv"), 1)

            def copy_expo_t1(s):
                need(dve, "expo_t_ps", s.n)
                dve.tensor_copy(expo_t[:, 2:4, :], F[3][:, :].rearrange("p (t n) -> p t n", t=tiles))\
                    .then_inc(sem("expo_t1"), 1)

            def residual2(s):
                need(dve, "att", s.n)
                need(dve, "row_inv", s.n)
                for k in range(blocks):
                    op = dve.scalar_tensor_tensor(out=z[2][:, k, :], in0=block_of(F[0], k),
                                                  scalar=row_inv[:, k:k + 1], in1=x2[:, k, :],
                                                  op0=ALU.mult, op1=ALU.add)
                op.then_inc(sem("z2"), 1)
                need(dve, "z2", s.n)
                statistics(2, lambda i: z[2][:, i, :], s)

            def norm2(s):
                normalize(2, x3, lambda i: z[2][:, i, :], s, "x3")

            def reset_state(c):
                need(dve, "tr", c.n)
                dve.tensor_scalar(reset[:, :], tr[:, :], 0.5, 0.5, ALU.mult, ALU.add)\
                    .then_inc(sem("reset"), 1)
                need(dve, "reset", c.n)
                dve.scalar_tensor_tensor(out=gated[:, :], in0=B[1][:, :], scalar=vcol("hh_n"),
                                         in1=reset[:, :], op0=ALU.add, op1=ALU.mult)\
                    .then_inc(sem("gated"), 1)
                need(dve, "gin_ps", c.n)
                need(dve, "gated", c.n)
                dve.tensor_tensor(new_pre[:, :], B[0][:, :], gated[:, :], ALU.add)\
                    .then_inc(sem("new_pre"), 1)

            def mix(c):
                need(dve, "x_less_new", c.n)
                need(dve, "tz", c.n)
                dve.scalar_tensor_tensor(out=mixed[:, :], in0=tz[:, :], scalar=1.0, in1=x_less_new[:, :],
                                         op0=ALU.add, op1=ALU.mult).then_inc(sem("mixed"), 1)
                need(dve, "x_plus_new", c.n)
                need(dve, "mixed", c.n)
                dve.scalar_tensor_tensor(out=y3t[:, :], in0=mixed[:, :], scalar=0.5,
                                         in1=x_plus_new[:, :], op0=ALU.mult, op1=ALU.add)\
                    .then_inc(sem("y3t"), 1)

            def statistics3(d):
                need(dve, "y3_ps", d.n)
                statistics(3, lambda i: block_of(B[0], i), d)

            def norm3(d):
                need(dve, "stored", d.prev_dma)
                normalize(3, out_sb, lambda i: block_of(B[0], i), d, "out_rows")

            def steps(f, s, c, d):
                do(split_x3, c)
                do(residual1, s)
                do(statistics3, d)
                do(split_hc, c)
                do(square_s, c)
                do(norm1, s)
                do(norm3, d)
                do(residual0, f)
                do(weigh_adj, c)
                do(norm0, f)
                do(weigh_scores, s)
                do(invert_sums, s)
                do(low_nm, c)
                do(copy_expo_t1, s)
                do(residual2, s)
                do(norm2, s)
                do(pre_xc, c)
                do(split_xc, c)
                do(reset_state, c)
                do(mix, c)

            over_pairs(dve, steps)

        @block.tensor
        def _(pe):
            pe.wait_ge(sem("params"), 16 * 6)
            pe.wait_ge(sem("pool_init"), 4)
            pe.wait_ge(sem("self_diag"), 1)
            pe.wait_ge(sem("bias_parts"), 1)
            pe.wait_ge(sem("w_parts"), 1)

            def add_bias(bank, name):
                n = BIAS_ROWS.index(name)
                pe.matmul(bank[:, :].rearrange("p (k c) -> p k c", k=blocks), ones_rows[:, :], bias_parts[:, n:n + 1, :].broadcast_to([FEATS, blocks, P]),
                          start=True, stop=False, skip_group_check=True)

            def split(bank, w_at, high, low, start, stop):
                for n, (w, part) in enumerate(((w_hi, high), (w_hi, low), (w_lo, high))):
                    op = pe.matmul(bank, block_of(w, w_at), part, start=start and n == 0, stop=stop and n == 2)
                return op

            def transposes(bank, src):
                for k in range(blocks):
                    op = pe.transpose(block_of(bank, k), src[:, k, :], ident[:, :])
                return op

            def weigh_nodes(bank, rows, weights, diag=None):
                for g in range(2):
                    for t in range(tiles):
                        op = pe.matmul(bank[:, g * nodes:(g + 1) * nodes], rows[:, tiles * g + t, :],
                                       weights[:, tiles * g + t, :], start=(t == 0),
                                       stop=(t == tiles - 1 and diag is None), skip_group_check=True)
                    if diag is not None:
                        for t in range(tiles):
                            op = pe.matmul(block_of(bank, tiles * g + t), rows[:, tiles * g + t, :],
                                           diag[:, :], start=False, stop=True, skip_group_check=True)
                return op

            conv = [(tap, n) for tap in range(taps) for n in range(3)]

            def conv2(lo, hi):
                for at in range(lo, hi):
                    tap, n = conv[at]
                    w, part = ((w_hi, hch), (w_hi, hcl), (w_lo, hch))[n]
                    op = pe.matmul(B[0][:, :].rearrange("p (g n) -> p g n", g=2), block_of(w, C2 + tap),
                                   part[:, :, tap:tap + nodes], start=(at == 0), stop=(at == len(conv) - 1))
                return op

            def layer0_nodes(f):
                need(pe, "x_in", f.dma)
                need(pe, "adjt_in", f.dma)
                need(pe, "u1c", f.prev)
                weigh_nodes(F[2], x_in, adjt_in).then_inc(sem("u0_ps"), 1)

            def layer0_channels(f):
                need(pe, "u0", f.n)
                need(pe, "z1", f.prev)
                add_bias(F[3], "b0")
                for k in range(blocks):
                    op = pe.matmul(block_of(F[3], k), block_of(u0, k), w0_sb[:, :], start=False,
                                   stop=True, skip_group_check=True)
                op.then_inc(sem("y0"), 1)

            def layer1_nodes(f):
                need(pe, "x1", f.n)
                need(pe, "expo_t0", f.prev)
                weigh_nodes(F[2], x1, adjt_in, self_diag).then_inc(sem("u1_ps"), 1)

            def layer1_hidden(f):
                need(pe, "u1c", f.n)
                need(pe, "z2", f.prev)
                for j in range(2):
                    op = pe.matmul(F[j][:, :], block_of(w1_sb, j), u1[:, :], start=True, stop=True)
                    op.then_inc(sem(f"h1_ps{j}"), 1)

            def layer1_out(f):
                need(pe, "h1_0", f.n)
                need(pe, "h1_1", f.n)
                need(pe, "expo_t1", f.prev)
                add_bias(F[3], "b2")
                for k in range(blocks):
                    for j in range(2):
                        op = pe.matmul(block_of(F[3], k), h1[:, j, k * P:(k + 1) * P], w2_sb[:, j, :],
                                       start=False, stop=(j == 1), skip_group_check=True)
                op.then_inc(sem("y1"), 1)

            def turn_x2(s):
                need(pe, "x2", s.n)
                transposes(F[2], x2).then_inc(sem("x2t_ps"), 1)

            def queries(s):
                need(pe, "x2t", s.n)
                pe.matmul(F[2][:, :], watt_sb[:, :], x2t[:, :], start=True, stop=True)\
                    .then_inc(sem("q_ps"), 1)

            def scores(s):
                need(pe, "q", s.n)
                need(pe, "mask_neg", s.n)
                for g in range(2):
                    pe.matmul(F[g][:, :].rearrange("p (t n) -> p t n", t=tiles), first_row[:, :],
                              mask_neg[:, g:g + 1, :].broadcast_to([P, tiles, nodes]), start=True,
                              stop=False, skip_group_check=True)
                    for t in range(tiles):
                        op = pe.matmul(F[g][:, t * nodes:(t + 1) * nodes], block_of(q, tiles * g + t),
                                       x2t[:, g * nodes:(g + 1) * nodes], start=False, stop=True,
                                       skip_group_check=True)
                op.then_inc(sem("scores"), 1)

            def turn_expo(s, z0):
                need(pe, "expo", s.n)
                if z0 is not None:
                    need(pe, "z0", z0.n)
                for g in range(2):
                    for t in range(tiles):
                        for i in range(tiles):
                            at = t * nodes + i * P
                            op = pe.transpose(F[2 + g][:, at:at + P],
                                              expo[:, tiles * g + i, t * P:(t + 1) * P], ident[:, :])
                op.then_inc(sem("expo_t_ps"), 1)

            def attend(s):
                need(pe, "expo_t0", s.n)
                need(pe, "expo_t1", s.n)
                for g in range(2):
                    for i in range(tiles):
                        for t in range(tiles):
                            op = pe.matmul(block_of(F[0], tiles * g + i),
                                           expo_t[:, tiles * g + t, i * P:(i + 1) * P],
                                           x2[:, tiles * g + t, :], start=(t == 0),
                                           stop=(t == tiles - 1), skip_group_check=True)
                op.then_inc(sem("att"), 1)

            def turn_x3(c):
                need(pe, "x3", c.n)
                need(pe, "gated", c.prev)
                transposes(B[1], x3).then_inc(sem("x3t_ps"), 1)

            def conv1_and_s(c):
                need(pe, "x3_parts", c.n)
                need(pe, "tr", c.prev)
                split(B[2][:, :], C1, x3h[:, :], x3l[:, :], True, True).then_inc(sem("conv1"), 1)
                need(pe, "tz", c.prev)
                split(B[3][:, :], SE, x3h[:, :], x3l[:, :], True, True).then_inc(sem("s_ps"), 1)

            def messages(c):
                add_bias(B[1], "b_msg")
                for k in range(blocks):
                    op = pe.matmul(block_of(B[1], k), block_of(x3t, k), wmsg_sb[:, :], start=False,
                                   stop=True, skip_group_check=True)
                op.then_inc(sem("msg_ps"), 1)

            def distances(c):
                need(pe, "feat_l", c.n)
                need(pe, "feat_sq", c.n)
                need(pe, "feat_r", c.n)
                need(pe, "hc", c.n)
                for g in range(2):
                    for t in range(tiles):
                        op = pe.matmul(B[2 + g][:, t * nodes:(t + 1) * nodes],
                                       feat_l[:, (tiles * g + t) * P:(tiles * g + t + 1) * P],
                                       feat_r[:, g * nodes:(g + 1) * nodes], start=True, stop=True,
                                       skip_group_check=True)
                op.then_inc(sem("dist"), 1)

            def conv2_part(lo, hi):
                def step(c):
                    if lo == 0:
                        need(pe, "hc_parts", c.n)
                        need(pe, "out_rows", c.prev)
                    op = conv2(lo, hi)
                    if hi == len(conv):
                        op.then_inc(sem("conv2"), 1)
                return step

            def message_sums(c):
                need(pe, "msg", c.n)
                need(pe, "adj_near", c.n)
                weigh_nodes(B[1], msg, adj_near).then_inc(sem("nmp"), 1)

            def gru_without_conv(c):
                need(pe, "nm_parts", c.n)
                split(B[1][:, :], HH + 2, x3h[:, :], x3l[:, :], True, True)
                for gate in range(2):
                    bank = B[2 + gate][:, :]
                    split(bank, HH + gate, x3h[:, :], x3l[:, :], True, False)
                    split(bank, IH + 3 + gate, nmh[:, :], nml[:, :], False, False)

            def gru_conv(c):
                need(pe, "xc_parts", c.n)
                for gate in range(2):
                    op = split(B[2 + gate][:, :], IH + gate, xch[:, :], xcl[:, :], False, True)
                op.then_inc(sem("gates_ps"), 1)
                split(B[0][:, :], IH + 2, xch[:, :], xcl[:, :], True, False)
                split(B[0][:, :], IH + 5, nmh[:, :], nml[:, :], False, True).then_inc(sem("gin_ps"), 1)

            def turn_y3(d):
                need(pe, "y3t", d.n)
                for k in range(blocks):
                    op = pe.transpose(block_of(B[0], k), block_of(y3t, k), ident[:, :])
                op.then_inc(sem("y3_ps"), 1)

            def steps(f, s, c, d):
                do(turn_x3, c)
                do(layer0_nodes, f)
                do(turn_y3, d)
                do(conv1_and_s, c)
                do(layer0_channels, f)
                do(messages, c)
                do(distances, c)
                do(turn_x2, s)
                do(conv2_part(0, 6), c)
                do(queries, s)
                do(conv2_part(6, 12), c)
                do(scores, s)
                do(message_sums, c)
                do(conv2_part(12, 27), c)
                do(lambda s: turn_expo(s, f), s)
                do(conv2_part(27, 33), c)
                do(attend, s)
                do(conv2_part(33, len(conv)), c)
                do(layer1_nodes, f)
                do(gru_without_conv, c)
                do(gru_conv, c)
                do(layer1_hidden, f)
                do(layer1_out, f)

            over_pairs(pe, steps)


def kernel(**inputs):
    import numpy as np
    import concourse.bacc as bacc
    from concourse import mybir as _mybir
    from concourse.bass_utils import run_bass_kernel_spmd as run

    a = {n: np.asarray(v) for n, v in inputs.items()}
    ch = a["x"].shape[-1]
    f32 = np.float32

    def spread(v, starts=(S_ROWS, SQ_ROWS, ONE_ROWS)):
        to = np.zeros((P,) + v.shape[1:], f32)
        for s in starts:
            to[s:s + v.shape[0]] = v
        return to

    columns = {
        "prelu_a": np.broadcast_to(a["L0_gnn_prelu_a"].reshape(1), (ch,)),
        "eps": np.broadcast_to(a["L1_gnn_eps"], (ch,)),
        "b1_lo": a["L1_gnn_b1"][:ch], "b1_hi": a["L1_gnn_b1"][ch:],
        "b_se": spread(a["L3_gnn_b_se"]),
        **{f"bn{n}_{k}": a[f"L3_gnn_bn{n}_{k}"] for n in (1, 2) for k in "gbmv"},
        **{f"{w}_{g}": a[f"L3_gnn_b_{w}"][i * ch:(i + 1) * ch] for w in ("ih", "hh") for i, g in enumerate("rzn")},
    }
    w_ih = a["L3_gnn_w_ih"].reshape(3, ch, 2, ch).transpose(3, 2, 0, 1).reshape(ch, 6, ch)
    w_hh = a["L3_gnn_w_hh"].reshape(3, ch, ch).transpose(2, 0, 1)
    arrays = {
        "x": a["x"], "adj": a["adj"], "adj_t": a["adj"].transpose(0, 2, 1), "mask": a["nodemask"],
        "vecs": np.stack([columns[n] for n in VEC], axis=1),
        "bias_rows": np.stack([a["L0_gnn_bias"], a["L1_gnn_b2"], a["L3_gnn_b_msg"]]),
        "w0": a["L0_gnn_W"], "w1": a["L1_gnn_W1"], "w2": a["L1_gnn_W2"], "w_att": a["L2_gnn_W"],
        "w_se": spread(a["L3_gnn_w_se"]).T, "w_conv1": a["L3_gnn_conv1_w"][:, :, 0].T,
        "w_conv2": a["L3_gnn_conv2_w"].transpose(1, 2, 0), "w_msg": a["L3_gnn_w_msg"].T,
        "w_ih": w_ih, "w_hh": w_hh,
    }
    nc = bacc.Bacc("TRN2", target_bir_lowering=False, num_devices=1)
    feeds, aps = {}, []
    for name, v in arrays.items():
        v = np.ascontiguousarray(v)
        feeds[f"in_{name}"] = v
        aps.append(nc.dram_tensor(f"in_{name}", v.shape, _mybir.dt.from_np(v.dtype), kind="ExternalInput").ap())
    aps.append(nc.dram_tensor("out_x", a["x"].shape, _mybir.dt.float32, kind="ExternalOutput").ap())
    adjacency_block_kernel(nc, *aps)
    return run(nc, [feeds], core_ids=[0]).results[0]["out_x"]
```

```python
from contextlib import ExitStack

import concourse.bass as bass
from concourse import mybir
from concourse.alu_op_type import AluOpType as ALU

ACT = mybir.ActivationFunctionType
F32 = mybir.dt.float32
F32R = mybir.dt.float32r
BF16 = mybir.dt.bfloat16
I32 = mybir.dt.int32

P = 128
EPS = 1e-5
MASKED = -1e30
LOWEST = -3.0e38

VEC = ["prelu_a", "eps", "b1_lo", "b1_hi", "b_se", "bn1_g", "bn1_b", "bn1_m", "bn1_v",
       "bn2_g", "bn2_b", "bn2_m", "bn2_v", "ih_r", "ih_z", "ih_n", "hh_r", "hh_z", "hh_n",
       "right0_a", "right0_b", "right1_a", "right1_b", "left0_a", "left0_b", "left1_a", "left1_b"]
V = {name: i for i, name in enumerate(VEC)}
BIAS_ROWS = ["b0", "b2", "b_msg"]
FACTORS = {"right0": ((1, 0), (1, 0), (0, 1)), "right1": ((0, 1), (1, 0), (0, 1)),
           "left0": ((-2, 0), (0, 1), (1, 0)), "left1": ((0, 1), (0, 1), (1, 0))}
GROUPS = (0, 32, 64)
FEATS = 96


def adjacency_block_kernel(nc, x, adj, adj_t, mask, vecs, bias_rows, w0, w1, w2, w_att, w_se, w_conv1,
                           w_conv2, w_msg, w_ih, w_hh, out):
    graphs, nodes, ch = x.shape
    pairs = graphs // 2
    blocks = 2 * nodes // P
    tiles = nodes // P
    cols = 2 * nodes
    taps = w_conv2.shape[1]
    pad = taps // 2
    half = nodes // 2
    last = half + pad - 1
    assert taps == 2 * pad + 1 and pad % 2 == 0 and ch == P and blocks == 4 and cols == 512

    x_d = x.rearrange("(k g) (t p) c -> k p (g t) c", g=2, p=P)
    adj_d = adj.rearrange("(k g) (t p) m -> k p (g t) m", g=2, p=P)
    adj_t_d = adj_t.rearrange("(k g) (t p) n -> k p (g t) n", g=2, p=P)
    mask_d = mask.rearrange("(k o g) n -> k o (g n)", g=2, o=1)
    out_d = out.rearrange("(k g) (t p) c -> k p (g t) c", g=2, p=P)

    with ExitStack() as ctx:
        def sb(name, shape, dt=F32):
            return ctx.enter_context(nc.sbuf_tensor(name, shape, dt))

        sems = {}

        def sem(name):
            if name not in sems:
                sems[name] = ctx.enter_context(nc.semaphore(name))
            return sems[name]

        def need(eng, name, count):
            if isinstance(count, int) and count <= 0:
                return
            eng.wait_ge(sem(name), count)

        def need_apart(eng, name, count):
            eng.wait_ge(sem("params"), 16)
            need(eng, name, count)

        class Pair:
            def __init__(self, eng, n):
                held = (lambda v: eng.snap(eng.to_reg(v))) if not isinstance(n, int) else (lambda v: v)
                self.n, self.prev = held(n), held(n - 1)
                self.dma, self.prev_dma = held(n * 16), held(n * 16 - 16)

        def do(step, pair):
            if pair is not None:
                step(pair)

        def over_pairs(eng, steps):
            def stages(e):
                steps(*(Pair(eng, e - k) if 1 <= e - k <= pairs else None for k in range(5)))

            for e in range(1, 6):
                stages(e)
            with eng.Fori(6, pairs + 1) as e:
                steps(*(Pair(eng, e - k) for k in range(5)))
            for e in range(pairs + 1, pairs + 5):
                stages(e)

        vec = sb("vec", [P, len(VEC)])
        w0_sb = sb("w0_sb", [P, P])
        w2_sb = sb("w2_sb", [P, 2, P])
        wmsg_sb = sb("wmsg_sb", [P, P])
        n_split = P * (1 + 1 + taps + 9 + 2 + 1 + pad)
        w_raw = sb("w_raw", [P, n_split])
        w_hi = sb("w_hi", [P, n_split], F32R)
        w_lo = sb("w_lo", [P, n_split], F32R)
        bias_raw = sb("bias_raw", [FEATS, 3, P])
        bias_rest = sb("bias_rest", [FEATS, 3, P])
        bias_hi = sb("bias_hi", [FEATS, 3, P], BF16)
        bias_mid = sb("bias_mid", [FEATS, 3, P], BF16)
        bias_parts = sb("bias_parts", [FEATS, 3, P], BF16)
        ident = sb("ident", [P, P])
        self_diag = sb("self_diag", [P, P])
        ones_rows = sb("ones_rows", [FEATS, P], BF16)
        first_row = sb("first_row", [P, P], BF16)
        bn1_scale = sb("bn1_scale", [P, 1])
        bn1_shift = sb("bn1_shift", [P, 1])
        bn2_scale = sb("bn2_scale", [P, 1])
        bn2_shift = sb("bn2_shift", [P, 1])
        bn_tmp = sb("bn_tmp", [P, 4])
        minus_half = sb("minus_half", [P, 4])
        one_minus_a = sb("one_minus_a", [P, 1])
        half_br = sb("half_br", [P, 1])
        half_bz = sb("half_bz", [P, 1])
        factor_bias = sb("factor_bias", [P, len(FACTORS)])

        x_in = sb("x_in", [P, blocks, P])
        adj_in = sb("adj_in", [P, blocks, nodes])
        adjt_in = sb("adjt_in", [P, blocks, nodes])
        adjt_h = sb("adjt_h", [P, blocks, nodes], F32R)
        adjt_l = sb("adjt_l", [P, blocks, nodes], F32R)
        x_in_h = sb("x_in_h", [P, blocks, P], F32R)
        x_in_l = sb("x_in_l", [P, blocks, P], F32R)
        diag_sum = sb("diag_sum", [P, blocks, P])
        mask_in = sb("mask_in", [P, cols], I32)
        unmasked = sb("unmasked", [P, 2, nodes])
        masked = sb("masked", [P, 2, nodes])
        mask_neg = sb("mask_neg", [P, 2, nodes], BF16)
        adj_m = sb("adj_m", [P, blocks, nodes])
        u0 = sb("u0", [P, cols])
        u1h = sb("u1h", [P, cols], F32R)
        u1l = sb("u1l", [P, cols], F32R)
        neg0 = sb("neg0", [P, cols])
        z = [sb(f"z{n}", [P, blocks, P]) for n in range(3)]
        res0 = z[0][:, :, :].rearrange("p k c -> p (k c)")
        x1 = sb("x1", [P, blocks, P])
        x2 = sb("x2", [P, blocks, P])
        x3 = sb("x3", [P, blocks, P])
        h1 = sb("h1", [P, 2, cols])
        x1h = sb("x1h", [P, blocks, P], F32R)
        x1l = sb("x1l", [P, blocks, P], F32R)
        x2th = sb("x2th", [P, cols], F32R)
        x2tl = sb("x2tl", [P, cols], F32R)
        qh = sb("qh", [P, cols], F32R)
        ql = sb("ql", [P, cols], F32R)
        prob = sb("prob", [P, blocks, nodes])
        expo = prob
        expo_t = sb("expo_t", [P, blocks, nodes])
        row_max = sb("row_max", [P, blocks])
        minus_max = sb("minus_max", [P, blocks])
        row_sum = sb("row_sum", [P, blocks])
        row_inv = sb("row_inv", [P, blocks])
        bn6 = sb("bn6", [P, 4, blocks, 6])
        stats = sb("stats", [P, 4, blocks, 2])
        var_eps = sb("var_eps", [P, 4, blocks])
        rstd = sb("rstd", [P, 4, blocks])
        shift = sb("shift", [P, 4, blocks])
        adjt_kept = sb("adjt_kept", [P, blocks, nodes])
        x3t = sb("x3t", [P, cols])
        x3t_kept = sb("x3t_kept", [P, cols])
        x3h = sb("x3h", [P, cols], F32R)
        x3l = sb("x3l", [P, cols], F32R)
        hc = sb("hc", [P, 2, half + pad, 2])
        diffs = [sb(f"diff{r}", [P, 2, half + pad]) for r in range(2)]
        conv_h = [sb(f"conv_h{n}", [P, 2, half + pad], F32R) for n in range(3)]
        conv_l = [sb(f"conv_l{n}", [P, 2, half + pad], F32R) for n in range(3)]
        factors = {name: sb(name, [FEATS, cols]) for name in FACTORS}
        feat_r = sb("feat_r", [FEATS, cols], F32R)
        feat_l = sb("feat_l", [FEATS, cols], F32R)
        msg = sb("msg", [P, blocks, P])
        near = sb("near", [P, blocks, nodes])
        adj_near = near
        nmh = sb("nmh", [P, cols], F32R)
        nml = sb("nml", [P, cols], F32R)
        xc_base = sb("xc_base", [P, cols])
        xch = sb("xch", [P, cols], F32R)
        xcl = sb("xcl", [P, cols], F32R)
        x_less_new = sb("x_less_new", [P, cols])
        x_plus_new = sb("x_plus_new", [P, cols])
        y3t = sb("y3t", [P, cols])
        out_sb = sb("out_sb", [P, blocks, P])

        xc_pre, xc, tr, tz, reset, gated, new_pre, new, mixed = (
            w_raw[:, n * cols:(n + 1) * cols] for n in range(9))

        F = [ctx.enter_context(nc.psum_tensor(f"front{n}", [P, 512], F32)) for n in range(4)]
        B = [ctx.enter_context(nc.psum_tensor(f"back{n}", [P, 512], F32)) for n in range(4)]

        def block_of(t, k):
            return t[:, k * P:(k + 1) * P]

        def by_parity(t):
            return t[:, :].rearrange("p (g n r) -> p g n r", g=2, r=2)

        def vcol(name):
            return vec[:, V[name]:V[name] + 1]

        W1, WA, SE, C1, C2, IH, HH, C2_SUM = 0, 2, 3, 4, 5, 5 + taps, 11 + taps, 14 + taps

        block = ctx.enter_context(nc.Block())

        @block.sync
        def _(sp):
            def load_x(f):
                need(sp, "x_in_parts", f.prev)
                need(sp, "res0", f.prev)
                sp.dma_start(x_in[:, :, :], x_d[f.prev]).then_inc(sem("x_in"), 16)

            def load_adjt(f):
                need(sp, "adjt_parts", f.prev)
                need(sp, "diag_sum", f.prev)
                sp.dma_start(adjt_in[:, :, :], adj_t_d[f.prev]).then_inc(sem("adjt_in"), 16)

            def load_mask_and_adj(f):
                need(sp, "adj_m", f.prev)
                sp.dma_start(mask_in[:, :], mask_d[f.prev].broadcast_to([P, cols])).then_inc(sem("mask_in"), 16)
                sp.dma_start(adj_in[:, :, :], adj_d[f.prev]).then_inc(sem("adj_in"), 16)

            def load_parameters():
                sp.dma_start(vec[:, :], vecs).then_inc(sem("params"), 16)
                for row in GROUPS:
                    sp.dma_start(bias_raw[row:row + 1, :, :],
                                 bias_rows.rearrange("(o r) c -> o r c", o=1)).then_inc(sem("bias_in"), 16)
                for dst, src in ((w0_sb[:, :], w0), (wmsg_sb[:, :], w_msg),
                                 (w2_sb[:, :, :], w2.rearrange("(j p) c -> p j c", p=P))):
                    sp.dma_start(dst, src).then_inc(sem("params"), 16)

            def load_weights():
                for at, src, count in ((W1, w1, 2), (WA, w_att, 1), (SE, w_se, 1), (C1, w_conv1, 1),
                                       (C2, w_conv2, taps), (IH, w_ih, 6), (HH, w_hh, 3)):
                    dst = w_raw[:, at * P:(at + count) * P]
                    if count > 1 and src is not w1:
                        dst = dst.rearrange("p (k c) -> p k c", k=count)
                    sp.dma_start(dst, src).then_inc(sem("weights_in"), 16)

            def load_adjt_kept(s):
                need(sp, "adj_near", s.prev)
                sp.dma_start(adjt_kept[:, :, :], adj_t_d[s.prev]).then_inc(sem("adjt_kept"), 16)

            def store(d):
                need(sp, "out_rows", d.n)
                sp.dma_start(out_d[d.prev], out_sb[:, :, :]).then_inc(sem("stored"), 16)

            def steps(e, f, s, c, d):
                do(load_mask_and_adj, f)
                do(load_adjt_kept, s)
                do(load_adjt, e)
                do(load_x, e)
                if f is None and e is not None:
                    load_parameters()
                    load_weights()
                do(store, d)

            over_pairs(sp, steps)
            sp.wait_ge(sem("stored"), 16 * pairs)

        @block.gpsimd
        def _(pool):
            pool.memset(ident[:, :], 0.0).then_inc(sem("pool_init"), 1)
            pool.memset(minus_half[:, :], -0.5)
            pool.memset(ones_rows[:, :], 1.0)
            pool.memset(first_row[:, :], 0.0)
            pool.memset(hc[:, :, :, :], 0.0).then_inc(sem("pool_init"), 1)
            pool.wait_ge(sem("pool_init"), 2)
            pool.memset(first_row[0:1, :], 1.0).then_inc(sem("pool_init"), 1)
            pool.affine_select(out=ident[:, :], in_=ident[:, :], compare_op=ALU.not_equal, fill=1.0,
                               base=0, pattern=[[-1, P]], channel_multiplier=1).then_inc(sem("pool_init"), 1)
            pool.wait_ge(sem("bn_var"), 1)
            pool.tensor_tensor(bn_tmp[:, 2:4], bn_tmp[:, 0:2], minus_half[:, 0:2], ALU.pow)\
                .then_inc(sem("bn_rstd"), 1)

            def masks(f):
                need_apart(pool, "mask_in", f.dma)
                need(pool, "soft_in", f.prev)
                pool.tensor_scalar(masked[:, :, :], mask_in[:, :].rearrange("p (g n) -> p g n", g=2),
                                   0.0, None, ALU.is_equal).then_inc(sem("masked"), 1)
                need_apart(pool, "masked", f.n)
                pool.tensor_scalar(unmasked[:, :, :], masked[:, :, :], -1.0, 1.0, ALU.mult, ALU.add)

            def mask_scores(f):
                pool.tensor_scalar(mask_neg[:, :, :], masked[:, :, :], MASKED, None, ALU.mult)\
                    .then_inc(sem("mask_neg"), 1)

            def sum_taps():
                pool.wait_ge(sem("weights_in"), 16 * 7)
                even_odd = w_raw[:, C2 * P:(C2 + 2 * pad) * P].rearrange("p (k r c) -> p k r c", r=2, c=P)
                pool.tensor_tensor(w_raw[:, C2_SUM * P:(C2_SUM + pad) * P].rearrange("p (k c) -> p k c", c=P),
                                   even_odd[:, :, 0, :], even_odd[:, :, 1, :], ALU.add).then_inc(sem("w_sums"), 1)

            def adjacency(f):
                need(pool, "mask_neg", f.n)
                need(pool, "adj_in", f.dma)
                for g in range(2):
                    at = slice(tiles * g, tiles * (g + 1))
                    keep = unmasked[:, g:g + 1, :].broadcast_to([P, tiles, nodes])
                    op = pool.tensor_tensor(adj_m[:, at, :], adj_in[:, at, :], keep, ALU.mult)
                op.then_inc(sem("adj_keep"), 1)
                need(pool, "adj_keep", f.n)
                for g in range(2):
                    at = slice(tiles * g, tiles * (g + 1))
                    fill = masked[:, g:g + 1, :].broadcast_to([P, tiles, nodes])
                    op = pool.tensor_tensor(adj_m[:, at, :], adj_m[:, at, :], fill, ALU.add)
                op.then_inc(sem("adj_m"), 1)

            def rsqrt(n):
                def step(k):
                    need(pool, f"var{n}", k.n)
                    pool.tensor_tensor(rstd[:, n, :], var_eps[:, n, :], minus_half[:, 0:blocks], ALU.pow)\
                        .then_inc(sem(f"rstd{n}"), 1)
                return step

            def low_inputs(f):
                need(pool, "adjt_high", f.n)
                pool.tensor_tensor(adjt_l[:, :, :], adjt_in[:, :, :], adjt_h[:, :, :].bitcast(F32),
                                   ALU.subtract).then_inc(sem("adjt_parts"), 1)
                need(pool, "x_in_high", f.n)
                pool.tensor_tensor(x_in_l[:, :, :], x_in[:, :, :], x_in_h[:, :, :].bitcast(F32),
                                   ALU.subtract).then_inc(sem("x_in_parts"), 1)

            def diagonal(f):
                pool.wait_ge(sem("self_diag"), 1)
                for k in range(blocks):
                    op = pool.tensor_tensor(diag_sum[:, k, :], block_of(adjt_in[:, k, :], k % tiles),
                                            self_diag[:, :], ALU.add)
                op.then_inc(sem("diag_sum"), 1)

            def multiply_factors(c):
                need(pool, "factors", c.n)
                for side in ("right", "left"):
                    first, second = factors[side + "0"], factors[side + "1"]
                    op = pool.tensor_tensor(first[:, :], first[:, :], second[:, :], ALU.mult)
                op.then_inc(sem("features"), 1)

            def low_x1(f):
                need(pool, "x1_high", f.n)
                pool.tensor_tensor(x1l[:, :, :], x1[:, :, :], x1h[:, :, :].bitcast(F32), ALU.subtract)\
                    .then_inc(sem("x1_parts"), 1)

            def low_diagonal(f):
                need(pool, "diag_high", f.n)
                for k in range(blocks):
                    op = pool.tensor_tensor(block_of(adjt_l[:, k, :], k % tiles), diag_sum[:, k, :],
                                            block_of(adjt_h[:, k, :], k % tiles).bitcast(F32),
                                            ALU.subtract)
                op.then_inc(sem("diag_parts"), 1)

            def around_new(c):
                need(pool, "new", c.n)
                need(pool, "x3t_kept", c.n)
                pool.tensor_tensor(x_less_new[:, :], x3t_kept[:, :], new[:, :], ALU.subtract)\
                    .then_inc(sem("x_less_new"), 1)
                pool.tensor_tensor(x_plus_new[:, :], x3t_kept[:, :], new[:, :], ALU.add)\
                    .then_inc(sem("x_plus_new"), 1)

            def steps(e, f, s, c, d):
                do(low_inputs, f)
                do(multiply_factors, c)
                do(around_new, d)
                do(diagonal, f)
                do(masks, f)
                if s is None and f is not None:
                    sum_taps()
                do(low_diagonal, f)
                do(rsqrt(0), f)
                do(rsqrt(3), d)
                do(low_x1, f)
                do(rsqrt(2), s)
                do(mask_scores, f)
                do(adjacency, f)
                do(rsqrt(1), f)

            over_pairs(pool, steps)

        @block.scalar
        def _(act):
            def high_first_weights():
                act.wait_ge(sem("weights_in"), 16 * 7)
                act.activation(w_hi[:, 0:SE * P], w_raw[:, 0:SE * P], ACT.Copy).then_inc(sem("w_high"), 1)
                act.wait_ge(sem("vectors"), 1)

            def high_last_weights():
                act.wait_ge(sem("w_sums"), 1)
                act.activation(w_hi[:, SE * P:n_split], w_raw[:, SE * P:n_split], ACT.Copy)\
                    .then_inc(sem("w_high"), 1)

            def copy_x3t(s):
                need(act, "x3t_ps", s.n)
                need(act, "xc_base", s.prev)
                act.activation(x3t[:, :], F[3][:, :], ACT.Copy).then_inc(sem("x3t"), 1)

            def copy_u0(f):
                need(act, "u0_ps", f.n)
                act.activation(u0[:, :], F[1][:, :], ACT.Copy).then_inc(sem("u0"), 1)

            def hidden_conv(c):
                need(act, "conv1", c.n)
                need(act, "diff1", c.prev)
                need(act, "odd_parts", c.prev)
                inner = slice(pad // 2, pad // 2 + half)
                act.activation(hc[:, :, inner, :], B[2][:, :].rearrange("p (g n r) -> p g n r", g=2, r=2),
                               ACT.Relu, bias=bn1_shift[:, :], scale=bn1_scale[:, :]).then_inc(sem("hc"), 1)

            def minus_part(f):
                need(act, "y0", f.n)
                act.activation(neg0[:, :], F[3][:, :], ACT.Relu, scale=-1.0).then_inc(sem("neg0"), 1)

            def features(c):
                need(act, "s_ps", c.n)
                need(act, "feat_low", c.prev)
                for n, name in enumerate(FACTORS):
                    op = act.activation(factors[name][:, :], B[3][0:FEATS, :], ACT.Identity,
                                        bias=factor_bias[0:FEATS, n:n + 1],
                                        scale=vec[0:FEATS, V[f"{name}_a"]:V[f"{name}_a"] + 1])
                op.then_inc(sem("factors"), 1)

            def high_features(c):
                need(act, "features", c.n)
                need(act, "dist", c.prev)
                act.activation(feat_r[:, :], factors["right0"][:, :], ACT.Copy)
                act.activation(feat_l[:, :], factors["left0"][:, :], ACT.Copy).then_inc(sem("feat_high"), 1)

            def relu_msg(c):
                need(act, "msg_ps", c.n)
                act.activation(msg[:, :, :], B[1][:, :].rearrange("p (k c) -> p k c", k=blocks),
                               ACT.Relu).then_inc(sem("msg"), 1)

            def nearness(c):
                need(act, "dist", c.n)
                for g in range(2):
                    act.activation(near[:, tiles * g:tiles * (g + 1), :],
                                   B[2 + g][:, :].rearrange("p (t n) -> p t n", t=tiles),
                                   ACT.Exp, scale=-1.0).then_inc(sem(f"near{g}"), 1)

            def keep_x3t(c):
                need(act, "x_plus_new", c.prev)
                act.activation(x3t_kept[:, :], x3t[:, :], ACT.Copy).then_inc(sem("x3t_kept"), 1)

            def high_adjt(f):
                need(act, "adjt_in", f.dma)
                need(act, "u1_ps", f.prev)
                act.activation(adjt_h[:, :, :], adjt_in[:, :, :], ACT.Copy).then_inc(sem("adjt_high"), 1)

            def high_x(f):
                need(act, "x_in", f.dma)
                need(act, "u0_ps", f.prev)
                act.activation(x_in_h[:, :, :], x_in[:, :, :], ACT.Copy).then_inc(sem("x_in_high"), 1)

            def high_diagonal(f):
                need(act, "diag_sum", f.n)
                need(act, "u0_ps", f.n)
                for g in range(2):
                    for t in range(tiles):
                        k = tiles * g + t
                        op = act.activation(block_of(adjt_h[:, k, :], t), diag_sum[:, k, :], ACT.Copy)
                op.then_inc(sem("diag_high"), 1)

            def scaled(n, dst, src, k, name):
                need(act, f"shift{n}", k.n)
                for i in range(blocks):
                    op = act.activation(dst[:, i, :], src(i), ACT.Identity, bias=shift[:, n, i:i + 1],
                                        scale=rstd[:, n, i:i + 1])
                op.then_inc(sem(name), 1)

            def norm0(f):
                need(act, "z1", f.prev)
                scaled(0, x1, lambda i: z[0][:, i, :], f, "x1")

            def high_x1(f):
                need(act, "x1", f.n)
                act.activation(x1h[:, :, :], x1[:, :, :], ACT.Copy).then_inc(sem("x1_high"), 1)

            def norm3(d):
                need(act, "stored", d.prev_dma)
                scaled(3, out_sb, lambda i: block_of(F[3], i), d, "out_rows")

            def high_u1(f):
                need(act, "u1_ps", f.n)
                act.activation(u1h[:, :], F[2][:, :], ACT.Copy).then_inc(sem("u1_high"), 1)

            def high_nm(c):
                need(act, "nmp", c.n)
                act.activation(nmh[:, :], B[1][:, :], ACT.Copy).then_inc(sem("nm_high"), 1)

            def hidden_channels(f):
                for j in range(2):
                    need(act, f"h1_ps{j}", f.n)
                    act.activation(h1[:, j, :], F[j][:, :], ACT.Relu,
                                   bias=vcol("b1_lo" if j == 0 else "b1_hi")).then_inc(sem(f"h1_{j}"), 1)

            def high_x2t(s):
                need(act, "x2t_ps", s.n)
                act.activation(x2th[:, :], F[2][:, :], ACT.Copy).then_inc(sem("x2t_high"), 1)

            def high_q(s):
                need(act, "q_ps", s.n)
                act.activation(qh[:, :], F[2][:, :], ACT.Copy).then_inc(sem("q_high"), 1)

            def relu_xc(c):
                need(act, "xc_pre", c.n)
                act.activation(xc[:, :], xc_pre[:, :], ACT.Relu, bias=bn2_shift[:, :])\
                    .then_inc(sem("xc"), 1)

            def exponentials(s):
                need(act, "soft_in", s.n)
                for k in range(blocks):
                    op = act.activation(expo[:, k, :], prob[:, k, :], ACT.Exp,
                                        bias=minus_max[:, k:k + 1], accum_out=row_sum[:, k:k + 1])
                op.then_inc(sem("expo"), 1)

            def copy_expo_t(s):
                need(act, "expo_t_ps", s.n)
                for g in range(2):
                    op = act.activation(expo_t[:, tiles * g:tiles * (g + 1), :],
                                        F[2 + g][:, :].rearrange("p (t n) -> p t n", t=tiles), ACT.Copy)
                op.then_inc(sem("expo_t"), 1)

            def gates(c):
                need(act, "gates_ps", c.n)
                act.activation(tr[:, :], B[2][:, :], ACT.Tanh, bias=half_br[:, :], scale=0.5)\
                    .then_inc(sem("tr"), 1)
                act.activation(tz[:, :], B[3][:, :], ACT.Tanh, bias=half_bz[:, :], scale=0.5)\
                    .then_inc(sem("tz"), 1)

            def new_state(c):
                need(act, "new_pre", c.n)
                act.activation(new[:, :], new_pre[:, :], ACT.Tanh, bias=vcol("ih_n"))\
                    .then_inc(sem("new"), 1)

            def steps(e, f, s, c, d):
                do(hidden_conv, c)
                do(features, c)
                do(relu_msg, c)
                do(high_x2t, s)
                do(new_state, d)
                do(high_q, s)
                do(high_features, c)
                do(copy_u0, f)
                do(nearness, c)
                do(keep_x3t, c)
                do(minus_part, f)
                if s is None and f is not None:
                    high_first_weights()
                do(exponentials, s)
                do(high_diagonal, f)
                do(high_nm, c)
                do(copy_expo_t, s)
                do(norm0, f)
                do(high_x1, f)
                do(norm3, d)
                do(relu_xc, c)
                if s is None and f is not None:
                    high_last_weights()
                do(high_u1, f)
                do(high_adjt, e)
                do(copy_x3t, s)
                do(high_x, e)
                do(hidden_channels, f)
                do(gates, c)

            over_pairs(act, steps)

        @block.vector
        def _(dve):
            dve.wait_ge(sem("params"), 16 * 4)
            for n, name in enumerate(("bn1_v", "bn2_v")):
                op = dve.tensor_scalar(bn_tmp[:, n:n + 1], vcol(name), EPS, None, ALU.add)
            op.then_inc(sem("bn_var"), 1)
            dve.tensor_scalar(one_minus_a[:, :], vcol("prelu_a"), -1.0, 1.0, ALU.mult, ALU.add)
            dve.tensor_tensor(half_br[:, :], vcol("ih_r"), vcol("hh_r"), ALU.add)
            dve.tensor_tensor(half_bz[:, :], vcol("ih_z"), vcol("hh_z"), ALU.add).then_inc(sem("dve_init"), 1)
            dve.wait_ge(sem("dve_init"), 1)
            dve.tensor_scalar(half_br[:, :], half_br[:, :], 0.5, None, ALU.mult)
            for n, name in enumerate(FACTORS):
                dve.scalar_tensor_tensor(out=factor_bias[:, n:n + 1], in0=vcol("b_se"), scalar=vcol(f"{name}_a"),
                                         in1=vcol(f"{name}_b"), op0=ALU.mult, op1=ALU.add)
            dve.tensor_scalar(half_bz[:, :], half_bz[:, :], 0.5, None, ALU.mult).then_inc(sem("dve_init"), 1)
            dve.wait_ge(sem("bn_rstd"), 1)
            dve.tensor_tensor(bn1_scale[:, :], vcol("bn1_g"), bn_tmp[:, 2:3], ALU.mult)
            dve.tensor_tensor(bn2_scale[:, :], vcol("bn2_g"), bn_tmp[:, 3:4], ALU.mult).then_inc(sem("dve_init"), 1)
            dve.wait_ge(sem("dve_init"), 3)
            dve.tensor_tensor(bn1_shift[:, :], vcol("bn1_m"), bn1_scale[:, :], ALU.mult)
            dve.tensor_tensor(bn2_shift[:, :], vcol("bn2_m"), bn2_scale[:, :], ALU.mult).then_inc(sem("dve_init"), 1)
            dve.wait_ge(sem("dve_init"), 4)
            dve.tensor_tensor(bn1_shift[:, :], vcol("bn1_b"), bn1_shift[:, :], ALU.subtract)
            dve.tensor_tensor(bn2_shift[:, :], vcol("bn2_b"), bn2_shift[:, :], ALU.subtract)\
                .then_inc(sem("vectors"), 1)
            dve.wait_ge(sem("pool_init"), 4)
            dve.tensor_scalar(self_diag[:, :], ident[:, :], vcol("eps"), None, ALU.mult).then_inc(sem("dve_init"), 1)
            dve.wait_ge(sem("dve_init"), 5)
            dve.tensor_tensor(self_diag[:, :], self_diag[:, :], ident[:, :], ALU.add).then_inc(sem("self_diag"), 1)
            dve.memset(bias_parts[:, :, :], 0.0).then_inc(sem("dve_init"), 1)
            dve.wait_ge(sem("bias_in"), 16 * 3)
            for row in GROUPS:
                op = dve.tensor_copy(bias_hi[row:row + 1, :, :], bias_raw[row:row + 1, :, :])
            op.then_inc(sem("dve_init"), 1)
            dve.wait_ge(sem("dve_init"), 7)
            dve.tensor_copy(bias_parts[0:1, :, :], bias_hi[0:1, :, :])
            for row in GROUPS[1:]:
                op = dve.tensor_tensor(bias_rest[row:row + 1, :, :], bias_raw[row:row + 1, :, :],
                                       bias_hi[row:row + 1, :, :], ALU.subtract)
            op.then_inc(sem("dve_init"), 1)
            dve.wait_ge(sem("dve_init"), 8)
            dve.tensor_copy(bias_parts[32:33, :, :], bias_rest[32:33, :, :])
            dve.tensor_copy(bias_mid[64:65, :, :], bias_rest[64:65, :, :]).then_inc(sem("dve_init"), 1)
            dve.wait_ge(sem("dve_init"), 9)
            dve.tensor_tensor(bias_parts[64:65, :, :], bias_rest[64:65, :, :], bias_mid[64:65, :, :],
                              ALU.subtract).then_inc(sem("bias_parts"), 1)

            def low_weights(part):
                at = (slice(0, SE * P), slice(SE * P, n_split))[part]
                dve.wait_ge(sem("w_high"), part + 1)
                dve.tensor_tensor(w_lo[:, at], w_raw[:, at], w_hi[:, at].bitcast(F32), ALU.subtract)\
                    .then_inc(sem("w_parts"), 1)

            def flat(t):
                return t[:, :, :].rearrange("p k c -> p (k c)")

            def moments(n, src):
                for i in range(blocks):
                    op = dve.bn_stats(bn6[:, n, i, :], src(i))
                op.then_inc(sem(f"bn6_{n}"), 1)

            def variances(n, k):
                need_apart(dve, f"bn6_{n}", k.n)
                for i in range(blocks):
                    op = dve.bn_aggr(stats[:, n, i, :], bn6[:, n, i, :])
                op.then_inc(sem(f"stats{n}"), 1)
                need(dve, f"stats{n}", k.n)
                dve.tensor_scalar(var_eps[:, n, :], stats[:, n, :, 1], EPS, None, ALU.add)\
                    .then_inc(sem(f"var{n}"), 1)

            def statistics(n, src, k):
                moments(n, src)
                variances(n, k)

            def normalize(n, dst, src, k, name):
                need(dve, f"rstd{n}", k.n)
                for i in range(blocks):
                    op = dve.tensor_scalar(dst[:, i, :], src(i), stats[:, n, i, 0:1], rstd[:, n, i:i + 1],
                                           ALU.subtract, ALU.mult)
                op.then_inc(sem(name), 1)

            def split_x3(s):
                need(dve, "x3t", s.n)
                need(dve, "state_ps", s.prev)
                dve.tensor_copy(x3h[:, :], x3t[:, :]).then_inc(sem("x3_high"), 1)
                need(dve, "x3_high", s.n)
                dve.tensor_tensor(x3l[:, :], x3t[:, :], x3h[:, :].bitcast(F32), ALU.subtract)\
                    .then_inc(sem("x3_parts"), 1)

            def residual0(f):
                need(dve, "neg0", f.n)
                dve.scalar_tensor_tensor(out=res0[:, :], in0=neg0[:, :], scalar=one_minus_a[:, :],
                                         in1=flat(x_in), op0=ALU.mult, op1=ALU.add).then_inc(sem("res0"), 1)
                need(dve, "res0", f.n)
                dve.tensor_tensor(flat(z[0]), F[3][:, :], res0[:, :], ALU.add).then_inc(sem("z0"), 1)
                need(dve, "z0", f.n)
                statistics(0, lambda i: z[0][:, i, :], f)

            def shift_of(n):
                def step(k):
                    need(dve, f"rstd{n}", k.n)
                    dve.scalar_tensor_tensor(out=shift[:, n, :], in0=stats[:, n, :, 0], scalar=-1.0,
                                             in1=rstd[:, n, :], op0=ALU.mult, op1=ALU.mult)\
                        .then_inc(sem(f"shift{n}"), 1)
                return step

            def low(name, part, src, high, k, ready):
                need(dve, ready, k.n)
                dve.tensor_tensor(part, src, high.bitcast(F32), ALU.subtract).then_inc(sem(name), 1)

            def low_u1(f):
                low("u1_parts", u1l[:, :], F[2][:, :], u1h[:, :], f, "u1_high")

            def low_x2t(s):
                low("x2t_parts", x2tl[:, :], F[2][:, :], x2th[:, :], s, "x2t_high")

            def low_q(s):
                low("q_parts", ql[:, :], F[2][:, :], qh[:, :], s, "q_high")

            def residual1(s):
                need(dve, "y1", s.n)
                dve.tensor_tensor(flat(z[1]), F[3][:, :], flat(x1), ALU.add).then_inc(sem("z1"), 1)

            def moments1(s):
                need(dve, "z1", s.n)
                moments(1, lambda i: z[1][:, i, :])

            def variances1(s):
                variances(1, s)

            def norm1(s):
                normalize(1, x2, lambda i: z[1][:, i, :], s, "x2")

            def high_odd(c):
                need(dve, "hc", c.n)
                dve.tensor_copy(conv_h[0][:, :, :], hc[:, :, :, 1]).then_inc(sem("odd_high"), 1)

            def low_odd(c):
                low("odd_parts", conv_l[0][:, :, :], hc[:, :, :, 1], conv_h[0][:, :, :], c, "odd_high")

            def differences(c):
                even, odd = hc[:, :, :, 0], hc[:, :, :, 1]
                dve.tensor_tensor(diffs[0][:, :, :], even, odd, ALU.subtract).then_inc(sem("diff0"), 1)
                dve.tensor_tensor(diffs[1][:, :, 0:last], even[:, :, 1:last + 1], odd[:, :, 0:last],
                                  ALU.subtract).then_inc(sem("diff1"), 1)

            def split_differences(c):
                need(dve, "conv2", c.prev)
                need(dve, "diff0", c.n)
                dve.tensor_copy(conv_h[1][:, :, :], diffs[0][:, :, :]).then_inc(sem("diff0_high"), 1)
                need(dve, "diff1", c.n)
                dve.tensor_copy(conv_h[2][:, :, 0:last], diffs[1][:, :, 0:last]).then_inc(sem("diff1_high"), 1)
                low("diff0_parts", conv_l[1][:, :, :], diffs[0][:, :, :], conv_h[1][:, :, :], c, "diff0_high")
                low("conv_parts", conv_l[2][:, :, 0:last], diffs[1][:, :, 0:last],
                    conv_h[2][:, :, 0:last], c, "diff1_high")

            def low_features(c):
                need(dve, "feat_high", c.n)
                for part, full, at in ((feat_r, factors["right0"], GROUPS[1]), (feat_l, factors["left0"], GROUPS[2])):
                    rows = slice(at, at + 32)
                    op = dve.tensor_tensor(part[rows, :], full[rows, :], part[rows, :].bitcast(F32), ALU.subtract)
                op.then_inc(sem("feat_low"), 1)

            def weigh_adj(c):
                need(dve, "adjt_kept", c.dma)
                for g in range(2):
                    need(dve, f"near{g}", c.n)
                    at = slice(tiles * g, tiles * (g + 1))
                    op = dve.tensor_tensor(adj_near[:, at, :], near[:, at, :], adjt_kept[:, at, :],
                                           ALU.mult)
                op.then_inc(sem("adj_near"), 1)

            def low_nm(c):
                need(dve, "nm_high", c.n)
                dve.tensor_tensor(nml[:, :], B[1][:, :], nmh[:, :].bitcast(F32), ALU.subtract)\
                    .then_inc(sem("nm_parts"), 1)

            def base_xc(c):
                need(dve, "conv_shared", c.n)
                shared = F[3][:, 0:2 * half].rearrange("p (g n o) -> p g n o", g=2, o=1)
                dve.scalar_tensor_tensor(out=by_parity(xc_base), in0=shared.broadcast_to([P, 2, half, 2]),
                                         scalar=bn2_scale[:, :], in1=by_parity(x3t), op0=ALU.mult,
                                         op1=ALU.add).then_inc(sem("xc_base"), 1)

            def pre_xc(c):
                need(dve, "conv2", c.n)
                need(dve, "xc_base", c.n)
                dve.scalar_tensor_tensor(out=by_parity(xc_pre), in0=B[0][:, :].rearrange(
                    "p (r g n) -> p g n r", g=2, r=2), scalar=bn2_scale[:, :], in1=by_parity(xc_base),
                    op0=ALU.mult, op1=ALU.add).then_inc(sem("xc_pre"), 1)

            def split_xc(c):
                need(dve, "xc", c.n)
                dve.tensor_copy(xch[:, :], xc[:, :]).then_inc(sem("xc_high"), 1)
                need(dve, "xc_high", c.n)
                dve.tensor_tensor(xcl[:, :], xc[:, :], xch[:, :].bitcast(F32), ALU.subtract)\
                    .then_inc(sem("xc_parts"), 1)

            def weigh_scores(s):
                need_apart(dve, "scores", s.n)
                need(dve, "adj_m", s.n)
                for k in range(blocks):
                    g, t = divmod(k, tiles)
                    op = dve.tensor_tensor_reduce(out=prob[:, k, :], in0=F[g][:, t * nodes:(t + 1) * nodes],
                                                  in1=adj_m[:, k, :], scale=1.0, scalar=LOWEST,
                                                  op0=ALU.mult, op1=ALU.max,
                                                  accum_out=row_max[:, k:k + 1])
                op.then_inc(sem("prob"), 1)
                need(dve, "prob", s.n)
                dve.tensor_scalar(minus_max[:, :], row_max[:, :], -1.0, None, ALU.mult)\
                    .then_inc(sem("soft_in"), 1)

            def invert_sums(s):
                need(dve, "expo", s.n)
                dve.reciprocal(row_inv[:, :], row_sum[:, :]).then_inc(sem("row_inv"), 1)

            def residual2(s):
                need(dve, "att", s.n)
                need(dve, "row_inv", s.n)
                for k in range(blocks):
                    op = dve.scalar_tensor_tensor(out=z[2][:, k, :], in0=block_of(F[0], k),
                                                  scalar=row_inv[:, k:k + 1], in1=x2[:, k, :],
                                                  op0=ALU.mult, op1=ALU.add)
                op.then_inc(sem("z2"), 1)

            def statistics2(s):
                need(dve, "z2", s.n)
                statistics(2, lambda i: z[2][:, i, :], s)

            def norm2(s):
                normalize(2, x3, lambda i: z[2][:, i, :], s, "x3")

            def reset_state(c):
                need(dve, "tr", c.n)
                dve.tensor_scalar(reset[:, :], tr[:, :], 0.5, 0.5, ALU.mult, ALU.add)\
                    .then_inc(sem("reset"), 1)
                need(dve, "reset", c.n)
                dve.scalar_tensor_tensor(out=gated[:, :], in0=B[1][:, :], scalar=vcol("hh_n"),
                                         in1=reset[:, :], op0=ALU.add, op1=ALU.mult)\
                    .then_inc(sem("gated"), 1)

            def add_new(c):
                need(dve, "gin_ps", c.n)
                need(dve, "gated", c.n)
                dve.tensor_tensor(new_pre[:, :], B[0][:, :], gated[:, :], ALU.add)\
                    .then_inc(sem("new_pre"), 1)

            def mix(c):
                need(dve, "x_less_new", c.n)
                need(dve, "tz", c.n)
                dve.scalar_tensor_tensor(out=mixed[:, :], in0=tz[:, :], scalar=1.0, in1=x_less_new[:, :],
                                         op0=ALU.add, op1=ALU.mult).then_inc(sem("mixed"), 1)
                need(dve, "x_plus_new", c.n)
                need(dve, "mixed", c.n)
                dve.scalar_tensor_tensor(out=y3t[:, :], in0=mixed[:, :], scalar=0.5,
                                         in1=x_plus_new[:, :], op0=ALU.mult, op1=ALU.add)\
                    .then_inc(sem("y3t"), 1)

            def statistics3(d):
                need(dve, "y3_ps", d.n)
                statistics(3, lambda i: block_of(F[3], i), d)

            def steps(e, f, s, c, d):
                do(moments1, s)
                do(high_odd, c)
                do(variances1, s)
                do(low_odd, c)
                do(differences, c)
                do(norm1, s)
                do(add_new, d)
                do(split_differences, c)
                do(base_xc, c)
                do(low_x2t, s)
                do(low_q, s)
                do(low_features, c)
                do(weigh_scores, s)
                do(weigh_adj, c)
                do(residual0, f)
                do(mix, d)
                do(low_nm, c)
                do(invert_sums, s)
                do(shift_of(0), f)
                do(statistics3, d)
                do(residual2, s)
                do(shift_of(3), d)
                do(statistics2, s)
                do(pre_xc, c)
                do(norm2, s)
                if s is None and f is not None:
                    low_weights(0)
                do(low_u1, f)
                if s is None and f is not None:
                    low_weights(1)
                do(split_xc, c)
                do(split_x3, s)
                do(reset_state, c)
                do(residual1, f)

            over_pairs(dve, steps)

        @block.tensor
        def _(pe):
            pe.wait_ge(sem("params"), 16 * 4)
            pe.wait_ge(sem("pool_init"), 4)
            pe.wait_ge(sem("bias_parts"), 1)

            def add_bias(bank, name):
                n = BIAS_ROWS.index(name)
                pe.matmul(bank[:, :].rearrange("p (k c) -> p k c", k=blocks), ones_rows[:, :],
                          bias_parts[:, n:n + 1, :].broadcast_to([FEATS, blocks, P]), start=True,
                          stop=False, skip_group_check=True)

            def split(bank, w_at, high, low, start, stop):
                for n, (w, part) in enumerate(((w_hi, high), (w_hi, low), (w_lo, high))):
                    op = pe.matmul(bank, block_of(w, w_at), part, start=start and n == 0, stop=stop and n == 2)
                return op

            def transposes(bank, src):
                for k in range(blocks):
                    op = pe.transpose(block_of(bank, k), src[:, k, :], ident[:, :])
                return op

            def weigh_nodes(bank, rows, weights):
                for g in range(2):
                    at = [(tiles * g + t, r, w) for t in range(tiles) for r, w in zip(rows, weights)]
                    for n, (k, r, w) in enumerate(at):
                        op = pe.matmul(bank[:, g * nodes:(g + 1) * nodes], r[:, k, :], w[:, k, :],
                                       start=(n == 0), stop=(n == len(at) - 1))
                return op

            shared = [(0, k, C2_SUM + k if k < pad else C2 + 2 * pad) for k in range(pad + 1)]
            even = [(1, k, C2 + 2 * k) for k in range(pad + 1)]
            odd = [(2, k, C2 + 2 * k + 1) for k in range(pad)]

            def conv_group(out, group, lo, hi):
                for at in range(lo, hi):
                    (which, k, w_at), n = group[at // 3], at % 3
                    w, part = ((w_hi, conv_h), (w_hi, conv_l), (w_lo, conv_h))[n]
                    op = pe.matmul(out.rearrange("p (g n) -> p g n", g=2), block_of(w, w_at),
                                   part[which][:, :, k:k + half], start=(at == 0),
                                   stop=(at == 3 * len(group) - 1), skip_group_check=True)
                return op

            def layer0_nodes(f):
                need(pe, "adjt_parts", f.n)
                need(pe, "x_in_parts", f.n)
                need(pe, "h1_1", f.prev)
                weigh_nodes(F[1], (x_in_h, x_in_h, x_in_l), (adjt_h, adjt_l, adjt_h))\
                    .then_inc(sem("u0_ps"), 1)

            def layer0_channels(f, c):
                need(pe, "u0", f.n)
                need(pe, "z1", f.prev)
                if c is not None:
                    need(pe, "xc_base", c.n)
                add_bias(F[3], "b0")
                for k in range(blocks):
                    op = pe.matmul(block_of(F[3], k), block_of(u0, k), w0_sb[:, :], start=False,
                                   stop=True, skip_group_check=True)
                op.then_inc(sem("y0"), 1)

            def layer1_nodes(f):
                need(pe, "x1_parts", f.n)
                need(pe, "diag_parts", f.n)
                need(pe, "expo_t", f.prev)
                weigh_nodes(F[2], (x1h, x1h, x1l), (adjt_h, adjt_l, adjt_h)).then_inc(sem("u1_ps"), 1)

            def layer1_hidden(f):
                pe.wait_ge(sem("w_parts"), 1)
                need(pe, "u1_parts", f.n)
                need(pe, "z2", f.prev)
                need(pe, "prob", f.prev)
                for j in range(2):
                    split(F[j][:, :], W1 + j, u1h[:, :], u1l[:, :], True, True).then_inc(sem(f"h1_ps{j}"), 1)

            def layer1_out(f):
                need(pe, "h1_0", f.n)
                need(pe, "h1_1", f.n)
                need(pe, "x3t", f.prev)
                add_bias(F[3], "b2")
                for k in range(blocks):
                    for j in range(2):
                        op = pe.matmul(block_of(F[3], k), h1[:, j, k * P:(k + 1) * P], w2_sb[:, j, :],
                                       start=False, stop=(j == 1), skip_group_check=True)
                op.then_inc(sem("y1"), 1)

            def turn_x2(s):
                need(pe, "x2", s.n)
                need(pe, "u1_parts", s.n)
                transposes(F[2], x2).then_inc(sem("x2t_ps"), 1)

            def queries(s):
                need(pe, "x2t_parts", s.n)
                split(F[2][:, :], WA, x2th[:, :], x2tl[:, :], True, True).then_inc(sem("q_ps"), 1)

            def scores(s, f):
                need(pe, "q_parts", s.n)
                need(pe, "mask_neg", s.n)
                for g in range(2):
                    if g == 1 and f is not None:
                        need(pe, "u0", f.n)
                    pe.matmul(F[g][:, :].rearrange("p (t n) -> p t n", t=tiles), first_row[:, :],
                              mask_neg[:, g:g + 1, :].broadcast_to([P, tiles, nodes]), start=True,
                              stop=False, skip_group_check=True)
                    for t in range(tiles):
                        for n, (qp, xp) in enumerate(((qh, x2th), (qh, x2tl), (ql, x2th))):
                            op = pe.matmul(F[g][:, t * nodes:(t + 1) * nodes],
                                           block_of(qp, tiles * g + t), xp[:, g * nodes:(g + 1) * nodes],
                                           start=False, stop=(n == 2), skip_group_check=True)
                op.then_inc(sem("scores"), 1)

            def turn_expo(s, f, c):
                need(pe, "expo", s.n)
                if f is not None:
                    need(pe, "z0", f.n)
                elif c is not None:
                    need(pe, "xc_base", c.n)
                for g in range(2):
                    for t in range(tiles):
                        for i in range(tiles):
                            at = t * nodes + i * P
                            op = pe.transpose(F[2 + g][:, at:at + P],
                                              expo[:, tiles * g + i, t * P:(t + 1) * P], ident[:, :])
                op.then_inc(sem("expo_t_ps"), 1)

            def attend(s):
                need(pe, "expo_t", s.n)
                for g in range(2):
                    for i in range(tiles):
                        for t in range(tiles):
                            op = pe.matmul(block_of(F[0], tiles * g + i),
                                           expo_t[:, tiles * g + t, i * P:(i + 1) * P],
                                           x2[:, tiles * g + t, :], start=(t == 0),
                                           stop=(t == tiles - 1), skip_group_check=True)
                op.then_inc(sem("att"), 1)

            def turn_x3(s, d):
                need(pe, "x3", s.n)
                if d is not None:
                    need(pe, "out_rows", d.n)
                transposes(F[3], x3).then_inc(sem("x3t_ps"), 1)

            def conv1_and_s(c):
                pe.wait_ge(sem("w_parts"), 2)
                need(pe, "x3_parts", c.n)
                need(pe, "tr", c.prev)
                split(B[2][:, :], C1, x3h[:, :], x3l[:, :], True, True).then_inc(sem("conv1"), 1)
                need(pe, "tz", c.prev)
                split(B[3][:, :], SE, x3h[:, :], x3l[:, :], True, True).then_inc(sem("s_ps"), 1)

            def messages(c):
                need(pe, "gated", c.prev)
                add_bias(B[1], "b_msg")
                for k in range(blocks):
                    op = pe.matmul(block_of(B[1], k), block_of(x3t, k), wmsg_sb[:, :], start=False,
                                   stop=True, skip_group_check=True)
                op.then_inc(sem("msg_ps"), 1)

            def distances(c):
                need(pe, "feat_low", c.n)
                need(pe, "hc", c.n)
                for g in range(2):
                    for t in range(tiles):
                        op = pe.matmul(B[2 + g][:, t * nodes:(t + 1) * nodes],
                                       feat_l[:, (tiles * g + t) * P:(tiles * g + t + 1) * P],
                                       feat_r[:, g * nodes:(g + 1) * nodes], start=True, stop=True,
                                       skip_group_check=True)
                op.then_inc(sem("dist"), 1)

            def conv_shared(c, s):
                need(pe, "odd_parts", c.n)
                if s is not None:
                    need(pe, "z1", s.n)
                conv_group(F[3][:, 0:2 * half], shared, 0, 3 * len(shared)).then_inc(sem("conv_shared"), 1)

            def conv_part(lo, hi):
                n_even = 3 * len(even)

                def step(c):
                    if lo == 0:
                        need(pe, "diff0_parts", c.n)
                        need(pe, "new_pre", c.prev)
                    if lo < n_even:
                        op = conv_group(B[0][:, 0:2 * half], even, lo, min(hi, n_even))
                    if hi > n_even:
                        if lo <= n_even:
                            need(pe, "conv_parts", c.n)
                        op = conv_group(B[0][:, 2 * half:cols], odd, max(lo - n_even, 0), hi - n_even)
                    if hi == conv_rest:
                        op.then_inc(sem("conv2"), 1)
                return step

            conv_rest = 3 * (len(even) + len(odd))

            def message_sums(c):
                need(pe, "msg", c.n)
                need(pe, "adj_near", c.n)
                weigh_nodes(B[1], (msg,), (adj_near,)).then_inc(sem("nmp"), 1)

            def gru_state(c):
                need(pe, "near1", c.n)
                for gate in range(2):
                    split(B[2 + gate][:, :], HH + gate, x3h[:, :], x3l[:, :], True, False)

            def gru_new_state(c):
                need(pe, "nm_parts", c.n)
                split(B[1][:, :], HH + 2, x3h[:, :], x3l[:, :], True, True).then_inc(sem("state_ps"), 1)

            def gru_messages(c):
                for gate in range(2):
                    split(B[2 + gate][:, :], IH + 3 + gate, nmh[:, :], nml[:, :], False, False)

            def gru_gates(c):
                need(pe, "xc_parts", c.n)
                for gate in range(2):
                    op = split(B[2 + gate][:, :], IH + gate, xch[:, :], xcl[:, :], False, True)
                op.then_inc(sem("gates_ps"), 1)

            def gru_new(c):
                split(B[0][:, :], IH + 2, xch[:, :], xcl[:, :], True, False)
                split(B[0][:, :], IH + 5, nmh[:, :], nml[:, :], False, True).then_inc(sem("gin_ps"), 1)

            def turn_y3(d, s, c):
                need(pe, "y3t", d.n)
                if s is not None:
                    need(pe, "expo_t", s.n)
                elif c is not None:
                    need(pe, "xc_base", c.n)
                need(pe, "out_rows", d.prev)
                for k in range(blocks):
                    op = pe.transpose(block_of(F[3], k), block_of(y3t, k), ident[:, :])
                op.then_inc(sem("y3_ps"), 1)

            def steps(e, f, s, c, d):
                do(conv1_and_s, c)
                do(gru_new, d)
                do(messages, c)
                do(lambda c: conv_shared(c, s), c)
                do(turn_x2, s)
                do(conv_part(0, 12), c)
                do(conv_part(12, 15), c)
                do(queries, s)
                do(layer0_nodes, f)
                do(lambda s: scores(s, f), s)
                do(distances, c)
                do(lambda f: layer0_channels(f, c), f)
                do(conv_part(15, 33), c)
                do(message_sums, c)
                do(lambda s: turn_expo(s, f, c), s)
                do(gru_state, c)
                do(lambda d: turn_y3(d, s, c), d)
                do(attend, s)
                do(gru_new_state, c)
                do(conv_part(33, conv_rest), c)
                do(layer1_nodes, f)
                do(gru_messages, c)
                do(lambda s: turn_x3(s, d), s)
                do(layer1_hidden, f)
                do(gru_gates, c)
                do(layer1_out, f)

            over_pairs(pe, steps)


def kernel(**inputs):
    import numpy as np
    import concourse.bacc as bacc
    from concourse import mybir as _mybir
    from concourse.bass_utils import run_bass_kernel_spmd as run

    a = {n: np.asarray(v) for n, v in inputs.items()}
    ch = a["x"].shape[-1]
    f32 = np.float32

    kinds = range(len(FACTORS["left0"]))
    dims = a["L3_gnn_w_se"].shape[0]
    assert len(kinds) * dims <= 32

    def spread(rows):
        to = np.zeros((P,) + rows[0].shape[1:], f32)
        for start in GROUPS:
            for kind in kinds:
                at = start + kind * dims
                to[at:at + dims] = rows[kind]
        return to

    def factor(name, n):
        return spread([np.full(dims, FACTORS[name][kind][n], f32) for kind in kinds])

    columns = {
        "prelu_a": np.broadcast_to(a["L0_gnn_prelu_a"].reshape(1), (ch,)),
        "eps": np.broadcast_to(a["L1_gnn_eps"], (ch,)),
        "b1_lo": a["L1_gnn_b1"][:ch], "b1_hi": a["L1_gnn_b1"][ch:],
        "b_se": spread([a["L3_gnn_b_se"]] * len(kinds)),
        **{f"{name}_{c}": factor(name, n) for name in FACTORS for n, c in enumerate("ab")},
        **{f"bn{n}_{k}": a[f"L3_gnn_bn{n}_{k}"] for n in (1, 2) for k in "gbmv"},
        **{f"{w}_{g}": a[f"L3_gnn_b_{w}"][i * ch:(i + 1) * ch] for w in ("ih", "hh") for i, g in enumerate("rzn")},
    }
    w_ih = a["L3_gnn_w_ih"].reshape(3, ch, 2, ch).transpose(3, 2, 0, 1).reshape(ch, 6, ch)
    w_hh = a["L3_gnn_w_hh"].reshape(3, ch, ch).transpose(2, 0, 1)
    arrays = {
        "x": a["x"], "adj": a["adj"], "adj_t": a["adj"].transpose(0, 2, 1), "mask": a["nodemask"],
        "vecs": np.stack([columns[n] for n in VEC], axis=1),
        "bias_rows": np.stack([a["L0_gnn_bias"], a["L1_gnn_b2"], a["L3_gnn_b_msg"]]),
        "w0": a["L0_gnn_W"], "w1": a["L1_gnn_W1"], "w2": a["L1_gnn_W2"], "w_att": a["L2_gnn_W"],
        "w_se": spread([a["L3_gnn_w_se"]] * len(kinds)).T, "w_conv1": a["L3_gnn_conv1_w"][:, :, 0].T,
        "w_conv2": a["L3_gnn_conv2_w"].transpose(1, 2, 0), "w_msg": a["L3_gnn_w_msg"].T,
        "w_ih": w_ih, "w_hh": w_hh,
    }
    nc = bacc.Bacc("TRN2", target_bir_lowering=False, num_devices=1)
    feeds, aps = {}, []
    for name, v in arrays.items():
        v = np.ascontiguousarray(v)
        feeds[f"in_{name}"] = v
        aps.append(nc.dram_tensor(f"in_{name}", v.shape, _mybir.dt.from_np(v.dtype), kind="ExternalInput").ap())
    aps.append(nc.dram_tensor("out_x", a["x"].shape, _mybir.dt.float32, kind="ExternalOutput").ap())
    adjacency_block_kernel(nc, *aps)
    return run(nc, [feeds], core_ids=[0]).results[0]["out_x"]
```
